# Optimizing a Trainium2 kernel written in Bass

```python
import numpy as np
import jax
import jax.numpy as jnp

def _softmax(x, axis=-1):
    return jax.nn.softmax(x, axis=axis)

def _gelu(x):
    return jax.nn.gelu(x, approximate=True)

def _silu(x):
    return jax.nn.silu(x)

def _sigmoid(x):
    return jax.nn.sigmoid(x)

def _layernorm(x, axis=-1, eps=1e-05):
    m = jnp.mean(x, axis=axis, keepdims=True)
    v = jnp.var(x, axis=axis, keepdims=True)
    return (x - m) / jnp.sqrt(v + eps)

def _scatter_add(tgt, idx, src, axis=0):
    return tgt.at[idx].add(src)

def _segment_sum(src, seg, n):
    return jax.ops.segment_sum(src, seg, n)
kernel_name = 'mk_adj_preln_d2_adj_r2_8a7747'

def setup_inputs(seed: int=0):
    np.random.seed(seed)
    _w = jnp.asarray

    def _rec_inputs():
        import jax
        import jax.numpy as jnp
        _gk = jax.random.key(seed)
        x = -5.207e-06 + 0.01001 * jax.random.normal(jax.random.fold_in(_gk, 1), (1354, 128), jnp.float32)
        _a = jax.random.bernoulli(jax.random.fold_in(_gk, 2), 0.0118168, (1354, 1354))
        _a = jnp.logical_or(_a, jnp.swapaxes(_a, -1, -2))
        _a = jnp.logical_or(_a, jnp.eye(1354, dtype=bool))
        _af = _a.astype(jnp.float32)
        _af = _af / jnp.maximum(_af.sum(-1, keepdims=True), 1.0)
        adj = _af
        return (x, adj)
    x, adj = _rec_inputs()

    def _L0_gnn_setup():
        import jax, jax.numpy as jnp
        import numpy as np
        MIN_NORM = 1e-15
        BALL_EPS = 0.004
        C_IN = 1.0
        C_OUT = 1.0

        def _norm(x):
            return jnp.clip(jnp.linalg.norm(x, axis=-1, keepdims=True), MIN_NORM, None)

        def artanh(x):
            return jnp.arctanh(jnp.clip(x, -1.0 + 1e-07, 1.0 - 1e-07))

        def proj(x, c):
            norm = _norm(x)
            maxnorm = (1.0 - BALL_EPS) / jnp.sqrt(c)
            return jnp.where(norm > maxnorm, x / norm * maxnorm, x)

        def expmap0(u, c):
            sc = jnp.sqrt(c)
            un = _norm(u)
            return jnp.tanh(sc * un) * u / (sc * un)

        def logmap0(p, c):
            sc = jnp.sqrt(c)
            pn = _norm(p)
            return artanh(sc * pn) * p / (sc * pn)

        def mobius_add(x, y, c):
            x2 = jnp.sum(x * x, -1, keepdims=True)
            y2 = jnp.sum(y * y, -1, keepdims=True)
            xy = jnp.sum(x * y, -1, keepdims=True)
            num = (1 + 2 * c * xy + c * y2) * x + (1 - c * x2) * y
            denom = 1 + 2 * c * xy + c * c * x2 * y2
            return num / jnp.clip(denom, MIN_NORM, None)

        def mobius_matvec(m, x, c):
            sc = jnp.sqrt(c)
            xn = _norm(x)
            mx = x @ m.T
            mxn = _norm(mx)
            res = jnp.tanh(mxn / xn * artanh(sc * xn)) * mx / (mxn * sc)
            zero_rows = jnp.all(mx == 0, axis=-1, keepdims=True)
            return jnp.where(zero_rows, jnp.zeros_like(res), res)
        key = jax.random.key(seed)
        k1, k2, k3, k4 = jax.random.split(key, 4)
        N, din, dout = (8192, 128, 128)
        x = jax.random.normal(k1, (N, din), dtype=jnp.float32) * 0.01
        adj = jax.random.uniform(k2, (N, N), dtype=jnp.float32)
        adj = adj / jnp.sum(adj, axis=-1, keepdims=True)
        bound = math_bound = float(np.sqrt(2.0) * np.sqrt(6.0 / (din + dout)))
        weight = jax.random.uniform(k3, (dout, din), dtype=jnp.float32, minval=-bound, maxval=bound)
        bias = jax.random.normal(k4, (dout,), dtype=jnp.float32) * 0.01
        return {'x': x, 'adj': adj, 'weight': weight, 'bias': bias}
    _L0_gnn_all = _L0_gnn_setup()
    _L0_gnn_in = {k: v for k, v in _L0_gnn_all.items() if k in ('weight', 'bias')}
    del _L0_gnn_all

    def _L1_gnn_setup():
        import jax, jax.numpy as jnp
        import numpy as np
        N = 512
        D = 128
        H = 8
        key = jax.random.key(seed)
        ks = jax.random.split(key, 7)
        s = (D * H) ** (-0.5)
        return {'x': jax.random.normal(ks[0], (N, D), dtype=jnp.float32), 'spatial_encoding': jax.random.normal(ks[1], (N, N), dtype=jnp.float32), 'edge_encoding': jax.random.normal(ks[2], (N, N), dtype=jnp.float32), 'Wq': jax.random.normal(ks[3], (D * H, D), dtype=jnp.float32) * s, 'Wk': jax.random.normal(ks[4], (D * H, D), dtype=jnp.float32) * s, 'Wv': jax.random.normal(ks[5], (D * H, D), dtype=jnp.float32) * s, 'Wo': jax.random.normal(ks[6], (D, D * H), dtype=jnp.float32) * s}
    _L1_gnn_all = _L1_gnn_setup()
    _L1_gnn_in = {k: v for k, v in _L1_gnn_all.items() if k in ('Wq', 'Wk', 'Wv', 'Wo')}
    del _L1_gnn_all
    return {'x': x, 'adj': adj, 'L0_gnn_weight': _L0_gnn_in['weight'], 'L0_gnn_bias': _L0_gnn_in['bias'], 'L1_gnn_Wq': _L1_gnn_in['Wq'], 'L1_gnn_Wk': _L1_gnn_in['Wk'], 'L1_gnn_Wv': _L1_gnn_in['Wv'], 'L1_gnn_Wo': _L1_gnn_in['Wo']}

def reference(x, adj, L0_gnn_weight, L0_gnn_bias, L1_gnn_Wq, L1_gnn_Wk, L1_gnn_Wv, L1_gnn_Wo):
    import jax
    import jax.numpy as jnp

    def _L0_gnn_ref(x, adj, weight, bias):
        import jax, jax.numpy as jnp
        import numpy as np
        MIN_NORM = 1e-15
        BALL_EPS = 0.004
        C_IN = 1.0
        C_OUT = 1.0

        def _norm(x):
            return jnp.clip(jnp.linalg.norm(x, axis=-1, keepdims=True), MIN_NORM, None)

        def artanh(x):
            return jnp.arctanh(jnp.clip(x, -1.0 + 1e-07, 1.0 - 1e-07))

        def proj(x, c):
            norm = _norm(x)
            maxnorm = (1.0 - BALL_EPS) / jnp.sqrt(c)
            return jnp.where(norm > maxnorm, x / norm * maxnorm, x)

        def expmap0(u, c):
            sc = jnp.sqrt(c)
            un = _norm(u)
            return jnp.tanh(sc * un) * u / (sc * un)

        def logmap0(p, c):
            sc = jnp.sqrt(c)
            pn = _norm(p)
            return artanh(sc * pn) * p / (sc * pn)

        def mobius_add(x, y, c):
            x2 = jnp.sum(x * x, -1, keepdims=True)
            y2 = jnp.sum(y * y, -1, keepdims=True)
            xy = jnp.sum(x * y, -1, keepdims=True)
            num = (1 + 2 * c * xy + c * y2) * x + (1 - c * x2) * y
            denom = 1 + 2 * c * xy + c * c * x2 * y2
            return num / jnp.clip(denom, MIN_NORM, None)

        def mobius_matvec(m, x, c):
            sc = jnp.sqrt(c)
            xn = _norm(x)
            mx = x @ m.T
            mxn = _norm(mx)
            res = jnp.tanh(mxn / xn * artanh(sc * xn)) * mx / (mxn * sc)
            zero_rows = jnp.all(mx == 0, axis=-1, keepdims=True)
            return jnp.where(zero_rows, jnp.zeros_like(res), res)
        mv = mobius_matvec(weight, x, C_IN)
        res = proj(mv, C_IN)
        hyp_bias = proj(expmap0(bias[None, :], C_IN), C_IN)
        h = proj(mobius_add(res, hyp_bias, C_IN), C_IN)
        xt = logmap0(h, C_IN)
        support_t = adj @ xt
        h = proj(expmap0(support_t, C_IN), C_IN)
        xt = jax.nn.relu(logmap0(h, C_IN))
        h = proj(expmap0(xt, C_OUT), C_OUT)
        return h

    def _L1_gnn_ref(x, spatial_encoding, edge_encoding, Wq, Wk, Wv, Wo):
        import jax, jax.numpy as jnp
        import numpy as np
        N = 512
        D = 128
        H = 8
        n, d = x.shape
        h = Wq.shape[0] // d
        scale = d ** (-0.5)
        q = (x @ Wq.T).reshape(d, n, h)
        k = (x @ Wk.T).reshape(d, n, h)
        v = (x @ Wv.T).reshape(d, n, h)
        a = jnp.einsum('dnh,dmh->dnm', q, k) * scale
        a = a + spatial_encoding + edge_encoding
        a = jax.nn.softmax(a, axis=2)
        out = jnp.einsum('dnm,dmh->dnh', a, v)
        out = out.reshape(n, h * d)
        return out @ Wo.T
    h = jnp.maximum(_layernorm(x, axis=-1), 0.0)
    x = x + _L0_gnn_ref(h, adj, L0_gnn_weight, L0_gnn_bias)
    h = jnp.maximum(_layernorm(x, axis=-1), 0.0)
    x = x + _L1_gnn_ref(h, adj, adj, L1_gnn_Wq, L1_gnn_Wk, L1_gnn_Wv, L1_gnn_Wo)
    return x

_drawn_inputs = setup_inputs


def setup_inputs(seed=0):
    import zlib

    import numpy as np

    out = dict(_drawn_inputs(seed))
    spreads = {}
    factors = {'L0_gnn_bias': 8.0, 'L1_gnn_Wq': 8.0, 'L1_gnn_Wk': 8.0}
    for name, (base, spread) in spreads.items():
        noise = np.random.default_rng([zlib.crc32(name.encode()), seed]).standard_normal(out[name].shape)
        drawn = base * np.exp(spread * noise) if base else spread * noise
        out[name] = jnp.asarray(drawn.astype(out[name].dtype))
    for name, factor in factors.items():
        out[name] = (out[name] * factor).astype(out[name].dtype)
    return out
```

```python
import concourse.bass as bass
from concourse import mybir
from contextlib import ExitStack

F32 = mybir.dt.float32
F16 = mybir.dt.float16
ALU = mybir.AluOpType
ACT = mybir.ActivationFunctionType
AX_X = mybir.AxisListType.X

N, D, H = 1354, 128, 8
P = 128
C = D * H
HEADS = D
FLAT = N * D
TILES = -(-N // P)
FULL = N // TILES
ROWS = FULL + 1
LASTROW = FULL * TILES
PADN = TILES * P
ADJW = TILES * ROWS
LN_EPS = 1e-5
MIN_NORM = 1e-15
MAX_NORM = 1.0 - 0.004
ARTANH_CLIP = 1.0 - 2.0 ** -23
ARTANH_MAX_NORM = 3.1063029
SCALE = float(D) ** -0.5

HALF = N // 2
BANK = 512
EXPW = 452
EXP_COLS = [(c * EXPW, min(EXPW, N - c * EXPW)) for c in range(3)]
SUMW = 339
SUM_COLS = [(c * SUMW, min(SUMW, N - c * SUMW)) for c in range(4)]
VROW = H + 1
LEAD = 3
LAG = 4
VEC_TILES = (1, 4, 7, 10)
POOL_TILES = tuple(t for t in range(TILES) if t not in VEC_TILES)
GROUPS = [(0, 4), (4, 4), (8, 3)]
QUARTER = BANK // D


def build_block(nc, x, adj_t, w0_t, bias, wqk, wv, wo, out):
    ctx = ExitStack()
    with ctx:
        def sb(name, shape, dt=F32):
            return ctx.enter_context(nc.sbuf_tensor(name, shape, dt))

        def ps(name, shape):
            return ctx.enter_context(nc.psum_tensor(name, shape, F32))

        def sem(name):
            return ctx.enter_context(nc.semaphore(name))

        q_split = nc.dram_tensor("q_split", (2 * H, FLAT), F16, kind="Internal").ap()
        k_split = nc.dram_tensor("k_split", (2 * H, FLAT), F16, kind="Internal").ap()
        v_rows = nc.dram_tensor("v_rows", (FLAT, VROW), F32, kind="Internal").ap()
        o_cols = nc.dram_tensor("o_cols", (VROW, FLAT), F32, kind="Internal").ap()
        adj_max_row = nc.dram_tensor("adj_max_row", (1, N), F32, kind="Internal").ap()

        adj_sb = sb("adj_sb", [P, TILES * ADJW])
        adj = adj_sb[:].rearrange("p (t n) -> p t n", t=TILES)
        ring = sb("ring", [P, 16384])
        probs = [ring[:, t * N:(t + 1) * N] for t in range(TILES)]
        rows_x = sb("rows_x", [P, TILES * D])
        row_t = sb("row_t", [P, TILES * ROWS])
        x_rows = rows_x[:].rearrange("p (t d) -> p t d", t=TILES)
        rows_t = row_t[:].rearrange("p (t r) -> p t r", t=TILES)
        work = [ring[:, i * 1536:(i + 1) * 1536].rearrange("p (t d) -> p t d", d=D) for i in range(3)]
        adj_max_b = sb("adj_max_b", [P, N])
        adj_tile_max = ring[:, 6144:6144 + ADJW]
        stage = [ring[:, b * 8192:(b + 1) * 8192].bitcast(F16)
                 .rearrange("p (w r c) -> p w r c", w=2, r=2 * H) for b in range(2)]
        v_stage = sb("v_stage", [P, 2, D * VROW])
        stat = sb("stat", [P, 24, TILES + 1])
        adj_row_max = sb("adj_row_max", [P, TILES])
        w0_sb = sb("w0_sb", [P, D])
        wqk_sb = sb("wqk_sb", [P, 2 * C])
        wv_sb = sb("wv_sb", [P, C])
        wo_sb = sb("wo_sb", [P, H * D])
        ident = sb("ident", [P, P])
        q_max = [sb(f"q_max{b}", [P, PADN], F16) for b in range(2)]
        k_max = [sb(f"k_max{b}", [P, PADN], F16) for b in range(2)]
        q_exp = [sb(f"q_exp{b}", [P, PADN], F16) for b in range(2)]
        k_exp = [sb(f"k_exp{b}", [P, PADN], F16) for b in range(2)]
        v_sb = [sb(f"v_sb{b}", [P, TILES * VROW]) for b in range(2)]
        half_max = [sb(f"half_max{b}", [P, TILES, 2]) for b in range(2)]
        neg_max = [sb(f"neg_max{b}", [P, TILES], F16) for b in range(2)]
        o_sb = [sb(f"o_sb{b}", [P, SUMW]) for b in range(2)]
        o_rows = adj_sb[:, 0:VROW * PADN].rearrange("p (h c) -> p h c", h=VROW)
        o_t = [ring[:, b * 1024:(b + 1) * 1024].rearrange("p (h r) -> p h r", h=H) for b in range(2)]
        recip_sum = ring[:, 2048:2048 + PADN]
        y_rows = ring[:, 4096:4096 + PADN].rearrange("p (t d) -> p t d", t=TILES)

        s_ps = ps("s_ps", [P, 4, BANK])
        t_ps = ps("t_ps", [P, 3, BANK])
        o_ps = ps("o_ps", [P, BANK])
        s_slot = [s_ps[:, 2 * b:2 * b + 2, :].rearrange("p b c -> p (b c)") for b in range(2)]
        proj_bank = [s_ps[:, b, :] for b in range(4)] + [t_ps[:, b, :] for b in range(3)]

        x_loaded, w0_loaded, w_loaded, adj_loaded = sem("x_loaded"), sem("w0_loaded"), sem("w_loaded"), sem("adj_loaded")
        ident_set, pads_zeroed, pads_set = sem("ident_set"), sem("pads_zeroed"), sem("pads_set")
        dve_step = sem("dve_step")
        stat_ready, stat_done = sem("stat_ready"), sem("stat_done")
        rows_ready, rows_turned, rows_t_ready = sem("rows_ready"), sem("rows_turned"), sem("rows_t_ready")
        mx_ready, xt_ready, support_ready = sem("mx_ready"), sem("xt_ready"), sem("support_ready")
        tile_max_ready, tile_max_turned, row_max_ready = sem("tile_max_ready"), sem("tile_max_turned"), sem("row_max_ready")
        row_max_stored, row_max_loaded = sem("row_max_stored"), sem("row_max_loaded")
        adj_shifted, e_ready = sem("adj_shifted"), sem("e_ready")
        proj_done, high_done, low_done = sem("proj_done"), sem("high_done"), sem("low_done")
        qk_stored = [sem(f"qk_stored{b}") for b in range(2)]
        v_stored = [sem(f"v_stored{b}") for b in range(2)]
        max_ops_loaded = [sem(f"max_ops_loaded{b}") for b in range(2)]
        exp_ops_loaded = [sem(f"exp_ops_loaded{b}") for b in range(2)]
        v_loaded = [sem(f"v_loaded{b}") for b in range(2)]
        neg_max_placed = [sem(f"neg_max_placed{b}") for b in range(2)]
        scores_ready, scores_maxed = sem("scores_ready"), sem("scores_maxed")
        neg_max_ready = sem("neg_max_ready")
        shifted_ready, exp_done = sem("shifted_ready"), sem("exp_done")
        vec_probs, pool_probs = sem("vec_probs"), sem("pool_probs")
        tile_summed, sums_copied = sem("tile_summed"), sem("sums_copied")
        sums_stored = [sem(f"sums_stored{b}") for b in range(2)]
        o_loaded, recip_ready, normed_v, normed_p = sem("o_loaded"), sem("recip_ready"), sem("normed_v"), sem("normed_p")
        o_turned, o_t_ready, y_ready, y_added, out_stored = sem("o_turned"), sem("o_t_ready"), sem("y_ready"), sem("y_added"), sem("out_stored")

        block = ctx.enter_context(nc.Block())

        def head_loop(eng, steps):
            for off in range(2):
                steps(0, off)
            with eng.Fori(1, HEADS // 2 - 1) as it:
                for off in range(2):
                    steps(it, off)
            for off in range(2):
                steps(HEADS // 2 - 1, off)

        def exists(it, off):
            return not isinstance(it, int) or 0 <= 2 * it + off < HEADS

        def head(it, off):
            return it * 2 + off

        def turn(it, off):
            return it + off // 2

        @block.sync
        def _(sp):
            sp.dma_start(x_rows[0:FULL, :, :], x[0:LASTROW, :].rearrange("(p t) d -> p t d", t=TILES)).then_inc(x_loaded, 16)
            sp.dma_start(x_rows[FULL:ROWS, :, :],
                         x[LASTROW:N, :].unsqueeze(1).to_broadcast([1, TILES, D])).then_inc(x_loaded, 16)
            sp.dma_start(w0_sb[:], w0_t).then_inc(w0_loaded, 16)
            sp.dma_start(work[0][0:ROWS, TILES, :], bias.to_broadcast([ROWS, D])).then_inc(w0_loaded, 16)
            for t0, t1 in ((0, 4), (4, 8), (8, TILES)):
                sp.dma_start(adj[0:FULL, t0:t1, 0:N],
                             adj_t[0:LASTROW, :].rearrange("(p t) n -> p t n", t=TILES)[:, t0:t1, :]).then_inc(adj_loaded, 16)
            sp.dma_start(adj[FULL:ROWS, :, 0:N],
                         adj_t[LASTROW:N, :].unsqueeze(1).to_broadcast([1, TILES, N])).then_inc(adj_loaded, 16)
            sp.dma_start(wqk_sb[:], wqk).then_inc(w_loaded, 16)
            sp.dma_start(wv_sb[:], wv).then_inc(w_loaded, 16)
            sp.dma_start(wo_sb[:], wo).then_inc(w_loaded, 16)

            sp.wait_ge(row_max_ready, 1)
            sp.dma_start(adj_max_row[0, 0:LASTROW].rearrange("(p t) -> p t", t=TILES), adj_row_max[0:FULL, :]).then_inc(row_max_stored, 16)
            sp.dma_start(adj_max_row[0:1, LASTROW:N], adj_row_max[FULL:ROWS, 0:1]).then_inc(row_max_stored, 16)
            sp.wait_ge(row_max_stored, 32)
            sp.dma_start(adj_max_b[0:ROWS, :], adj_max_row.to_broadcast([ROWS, N])).then_inc(row_max_loaded, 16)

            def flat_tiles(arr):
                return arr[:, 0:LASTROW * D].rearrange("r (p c) -> p r c", c=TILES * D)

            for g, (t0, nt) in enumerate(GROUPS):
                for t in range(t0, t0 + nt):
                    sp.wait_ge(high_done, 6 * t + 6)
                    row = v_rows.rearrange("(r j) c -> r (j c)", j=D)
                    sp.dma_start(row[0:LASTROW, :].rearrange("(p t) c -> p t c", t=TILES)[:, t, :],
                                 v_stage[0:FULL, t % 2, :]).then_inc(v_stored[t % 2], 16)
                    if t == 0:
                        sp.dma_start(row[LASTROW:N, :], v_stage[FULL:ROWS, 0, :]).then_inc(v_stored[0], 16)
                sp.wait_ge(low_done, 4 * (t0 + nt))
                for w, arr in enumerate((q_split, k_split)):
                    sp.dma_start(flat_tiles(arr)[:, :, t0 * D:(t0 + nt) * D],
                                 stage[g % 2][0:FULL, w, :, 0:nt * D]).then_inc(qk_stored[g % 2], 16)
                    if g == 0:
                        sp.dma_start(arr[:, LASTROW * D:FLAT].unsqueeze(0), stage[0][FULL:ROWS, w, :, 0:D]).then_inc(qk_stored[0], 16)
            sp.wait_ge(qk_stored[0], 96)
            sp.wait_ge(qk_stored[1], 32)
            sp.wait_ge(v_stored[0], 112)
            sp.wait_ge(v_stored[1], 80)

            def load_operands(q_dst, k_dst, it, off, signal):
                cols = bass.ds(head(it, off) * N, N)
                for i in range(2):
                    sp.dma_start(q_dst[2 * H * i:2 * H * (i + 1), 0:N], q_split[:, cols]).then_inc(signal, 16)
                    for j in range(2):
                        r = 2 * H * i + H * j
                        sp.dma_start(k_dst[r:r + H, 0:N], k_split[H * i:H * (i + 1), cols]).then_inc(signal, 16)

            def load_v(it, off):
                b, first = off % 2, head(it, off) * N
                src = v_rows[bass.ds(first, LASTROW), :].rearrange("(p t) c -> p (t c)", t=TILES)
                sp.dma_start(v_sb[b][0:FULL, :], src).then_inc(v_loaded[b], 16)
                sp.dma_start(v_sb[b][FULL:ROWS, 0:VROW], v_rows[bass.ds(first + LASTROW, 1), :]).then_inc(v_loaded[b], 16)

            def place_neg_max(b):
                sp.dma_start(q_exp[b][4 * H:4 * H + 1, 0:LASTROW], neg_max[b][0:FULL, :]).then_inc(neg_max_placed[b], 16)
                sp.dma_start(q_exp[b][4 * H:4 * H + 1, LASTROW:N], neg_max[b][FULL:ROWS, 0:1]).then_inc(neg_max_placed[b], 16)

            def store_sums(it, off):
                b = off % 2
                for c, (c0, w) in enumerate(SUM_COLS):
                    sp.dma_start(o_cols[:, bass.ds(head(it, off) * N + c0, w)],
                                 o_sb[b][32 * c:32 * c + VROW, 0:w]).then_inc(sums_stored[b], 16)

            sp.wait_ge(pads_set, 1)
            for off in range(2):
                load_operands(q_max[off], k_max[off], 0, off, max_ops_loaded[off])
            load_operands(q_exp[0], k_exp[0], 0, 0, exp_ops_loaded[0])
            load_v(0, 0)
            sp.wait_ge(neg_max_ready, 1)
            place_neg_max(0)

            def head_steps(it, off):
                b = off % 2
                if exists(it, off + 2):
                    sp.wait_ge(scores_ready, head(it, off) * (2 * TILES) + 2 * TILES)
                    load_operands(q_max[b], k_max[b], it, off + 2, max_ops_loaded[b])
                if exists(it, off + 1):
                    if exists(it, off - 1):
                        sp.wait_ge(shifted_ready, head(it, off) * (3 * TILES))
                    load_operands(q_exp[1 - b], k_exp[1 - b], it, off + 1, exp_ops_loaded[1 - b])
                    if exists(it, off - 1):
                        sp.wait_ge(tile_summed, head(it, off) * TILES)
                    load_v(it, off + 1)
                if exists(it, off - 1):
                    sp.wait_ge(sums_copied, head(it, off))
                    store_sums(it, off - 1)
                if exists(it, off + 1):
                    sp.wait_ge(neg_max_ready, head(it, off) + 2)
                    place_neg_max(1 - b)

            head_loop(sp, head_steps)
            sp.wait_ge(sums_copied, HEADS)
            store_sums(HEADS // 2 - 1, 1)
            for b in range(2):
                sp.wait_ge(sums_stored[b], 64 * (HEADS // 2))

            sp.dma_start(o_rows[0:FULL, :, :], flat_tiles(o_cols)).then_inc(o_loaded, 16)
            last = o_cols[:, LASTROW * D:FLAT].unsqueeze(0).unsqueeze(2).to_broadcast([1, VROW, TILES, D])
            sp.dma_start(o_rows[FULL:ROWS, :, :].rearrange("p h (t c) -> p h t c", t=TILES), last).then_inc(o_loaded, 16)
            sp.wait_ge(y_added, TILES)
            sp.dma_start(out[0:LASTROW, :].rearrange("(p t) d -> p t d", t=TILES), y_rows[0:FULL, :, :]).then_inc(out_stored, 16)
            sp.dma_start(out[LASTROW:N, :], y_rows[FULL:ROWS, 0, :]).then_inc(out_stored, 16)
            sp.wait_ge(out_stored, 32)

        @block.gpsimd
        def _(pool):
            nc.gpsimd.memset(ident[:], 0.0).then_inc(ident_set, 1)
            pool.wait_ge(ident_set, 1)
            nc.gpsimd.affine_select(out=ident[:], in_=ident[:], compare_op=ALU.not_equal, fill=1.0,
                                    base=0, pattern=[[-1, P]], channel_multiplier=1).then_inc(ident_set, 1)
            nc.gpsimd.memset(adj[:, :, N:ADJW], 0.0).then_inc(ident_set, 1)
            nc.gpsimd.memset(v_stage[:], 1.0).then_inc(ident_set, 1)
            for b in range(2):
                for buf in (q_max[b], k_max[b], q_exp[b], k_exp[b], v_sb[b], half_max[b]):
                    nc.gpsimd.memset(buf[:], 0.0).then_inc(pads_zeroed, 1)
            pool.wait_ge(pads_zeroed, 12)
            nc.gpsimd.memset(k_exp[0][4 * H:4 * H + 1, 0:N], 1.0).then_inc(pads_zeroed, 1)
            pool.wait_ge(pads_zeroed, 13)
            nc.gpsimd.memset(k_exp[1][4 * H:4 * H + 1, 0:N], 1.0).then_inc(pads_set, 1)

            pool.wait_ge(e_ready, TILES)

            def head_steps(it, off):
                for t in POOL_TILES:
                    pool.wait_ge(exp_done, head(it, off) * (3 * TILES) + 3 * (t + 1))
                    nc.gpsimd.tensor_tensor(probs[t][0:ROWS, :], probs[t][0:ROWS, :], adj[0:ROWS, t, 0:N],
                                            ALU.mult).then_inc(pool_probs, 1)

            head_loop(pool, head_steps)
            pool.wait_ge(recip_ready, 1)
            for h in (6, 7):
                nc.gpsimd.tensor_tensor(o_rows[0:ROWS, h, :], o_rows[0:ROWS, h, :], recip_sum[0:ROWS, :],
                                        ALU.mult).then_inc(normed_p, 1)

        @block.scalar
        def _(act):
            def row_stat(n, dst, src, func, **more):
                act.wait_ge(stat_ready, n)
                nc.scalar.activation(dst, src, func, **more).then_inc(stat_done, 1)

            A = slice(0, ROWS)
            row_stat(1, stat[A, 2, 0:TILES], stat[A, 1, 0:TILES], ACT.Sqrt)
            row_stat(2, stat[A, 1, 0:TILES], stat[A, 0, 0:TILES], ACT.Sqrt)
            row_stat(3, stat[A, 3, :], stat[A, 2, :], ACT.Sqrt)
            row_stat(4, stat[A, 8, 0:TILES], stat[A, 7, 0:TILES], ACT.Ln)
            row_stat(5, stat[A, 9, :], stat[A, 8, :], ACT.Tanh)
            row_stat(6, stat[A, 1, 0:TILES], stat[A, 0, 0:TILES], ACT.Sqrt)
            row_stat(7, stat[A, 8, 0:TILES], stat[A, 7, 0:TILES], ACT.Ln)
            row_stat(8, stat[A, 1, 0:TILES], stat[A, 0, 0:TILES], ACT.Sqrt)
            row_stat(9, stat[A, 1, 0:TILES], stat[A, 0, 0:TILES], ACT.Sqrt)
            row_stat(10, stat[A, 3, 0:TILES], stat[A, 2, 0:TILES], ACT.Tanh)
            row_stat(11, stat[A, 2, 0:TILES], stat[A, 1, 0:TILES], ACT.Sqrt)

            act.wait_ge(ident_set, 4)
            n = 0
            for t in range(TILES):
                g = [t >= t0 for t0, _ in GROUPS].count(True) - 1
                if t == GROUPS[2][0]:
                    act.wait_ge(qk_stored[0], 64)
                if t >= 2:
                    act.wait_ge(v_stored[t % 2], 16 * (t // 2) + 16 * (t % 2 == 0))
                for c in range(6):
                    act.wait_ge(proj_done, n + 1)
                    if c < 4:
                        dst = stage[g % 2][A, c // 2, 4 * (c % 2):4 * (c % 2) + 4, (t - GROUPS[g][0]) * D:(t - GROUPS[g][0] + 1) * D]
                        src = proj_bank[n % 7][A, :].rearrange("p (h j) -> p h j", j=D)
                    else:
                        dst = v_stage[A, t % 2, (c - 4) * 64 * VROW:(c - 3) * 64 * VROW].rearrange("p (j k) -> p j k", k=VROW)[:, :, 0:H]
                        src = proj_bank[n % 7][A, :].rearrange("p (j k) -> p j k", k=H)
                    nc.scalar.activation(dst, src, ACT.Copy).then_inc(high_done, 1)
                    n += 1
            for t in range(TILES):
                act.wait_ge(adj_shifted, t + 1)
                nc.scalar.activation(adj[A, t, 0:N], adj[A, t, 0:N], ACT.Exp, scale=2.0).then_inc(e_ready, 1)
            for b in range(2):
                act.wait_ge(qk_stored[b], (96, 32)[b])

            def head_steps(it, off):
                b = off % 2
                for i in range(TILES):
                    if exists(it, off - 1):
                        act.wait_ge(tile_summed, head(it, off) * TILES + (i + 1 - TILES))
                    for c, (c0, w) in enumerate(EXP_COLS):
                        act.wait_ge(shifted_ready, head(it, off) * (3 * TILES) + 3 * i + c + 1)
                        nc.scalar.activation(probs[i][A, c0:c0 + w], t_ps[A, c, 0:w], ACT.Exp, scale=SCALE).then_inc(exp_done, 1)
                        if i == LAG and c == 0 and exists(it, off - 1):
                            copy_sums(it, off - 1)

            def copy_sums(it, off):
                b = off % 2
                act.wait_ge(tile_summed, head(it, off) * TILES + TILES)
                if exists(it, off - 2):
                    act.wait_ge(sums_stored[b], turn(it, off) * 64)
                nc.scalar.activation(o_sb[b][:], o_ps[:, 0:SUMW], ACT.Copy).then_inc(sums_copied, 1)

            head_loop(act, head_steps)
            copy_sums(HEADS // 2 - 1, 1)

        @block.vector
        def _(dve):
            steps = [0]
            asked = [0]

            def link(ins):
                steps[0] += 1
                ins.then_inc(dve_step, 1)
                dve.wait_ge(dve_step, steps[0])

            def ask(ins):
                asked[0] += 1
                ins.then_inc(stat_ready, 1)
                dve.wait_ge(stat_done, asked[0])

            A = slice(0, ROWS)
            tt, ts, stt = nc.vector.tensor_tensor, nc.vector.tensor_scalar, nc.vector.scalar_tensor_tensor

            def st(i, n=TILES):
                return stat[A, i, 0:n]

            def wide(i, n=TILES):
                return st(i, n).unsqueeze(2).to_broadcast([ROWS, n, D])

            def layernorm_relu(src, dst, centred, square):
                link(nc.vector.reduce_sum(st(0), src, AX_X))
                link(ts(st(0), st(0), -1.0 / D, None, ALU.mult))
                link(tt(centred, src, wide(0), ALU.add))
                link(tt(square, centred, centred, ALU.mult))
                link(nc.vector.reduce_sum(st(1), square, AX_X))
                ask(ts(st(1), st(1), 1.0 / D, LN_EPS, ALU.mult, ALU.add))
                link(nc.vector.reciprocal(st(2), st(2)))
                return stt(out=dst, in0=centred, scalar=0.0, in1=wide(2), op0=ALU.max, op1=ALU.mult)

            def artanh(dst, z):
                link(ts(st(4), st(z), 1.0, None, ALU.add))
                link(ts(st(5), st(z), -1.0, 1.0, ALU.mult, ALU.add))
                link(nc.vector.reciprocal(st(6), st(5)))
                ask(tt(st(7), st(4), st(6), ALU.mult))
                link(tt(st(4), st(z), st(z), ALU.mult))
                link(ts(st(5), st(4), 1.0 / 7, 1.0 / 5, ALU.mult, ALU.add))
                link(tt(st(5), st(5), st(4), ALU.mult))
                link(ts(st(5), st(5), 1.0 / 3, None, ALU.add))
                link(tt(st(5), st(5), st(4), ALU.mult))
                link(ts(st(5), st(5), 1.0, None, ALU.add))
                link(tt(st(5), st(5), st(z), ALU.mult))
                link(ts(st(8), st(8), 0.5, None, ALU.mult))
                link(ts(st(6), st(z), 0.1, None, ALU.is_lt))
                link(tt(st(5), st(5), st(8), ALU.subtract))
                link(tt(st(5), st(5), st(6), ALU.mult))
                link(tt(st(dst), st(8), st(5), ALU.add))

            nc.vector.memset(o_ps[:], 0.0).then_inc(dve_step, 1)
            steps[0] += 1
            dve.wait_ge(x_loaded, 32)
            h0 = work[1][A, 0:TILES, :]
            sq = work[2][A, 0:TILES, :]
            layernorm_relu(x_rows[A], h0, h0, sq).then_inc(rows_ready, 1)
            dve.wait_ge(rows_ready, 1)
            link(tt(sq, h0, h0, ALU.mult))
            ask(nc.vector.reduce_sum(st(0), sq, AX_X))
            link(ts(st(10), st(1), MIN_NORM, None, ALU.max))
            dve.wait_ge(rows_turned, 1)
            for b in range(3):
                k = min(QUARTER, TILES - QUARTER * b)
                ins = nc.vector.tensor_copy(rows_t[:, QUARTER * b:QUARTER * b + k, :],
                                            s_ps[:, b, 0:k * D].rearrange("p (t r) -> p t r", r=D)[:, :, 0:ROWS])
            ins.then_inc(rows_t_ready, 1)

            dve.wait_ge(w0_loaded, 32)
            dve.wait_ge(mx_ready, 1)
            for b in range(3):
                k = min(QUARTER, TILES - QUARTER * b)
                link(nc.vector.tensor_copy(work[0][A, QUARTER * b:QUARTER * b + k, :],
                                           t_ps[A, b, 0:k * D].rearrange("p (t d) -> p t d", d=D)))
            ALLR = TILES + 1
            mx = work[0][A, 0:ALLR, :]
            sqa = work[2][A, 0:ALLR, :]
            link(tt(sqa, mx, mx, ALU.mult))
            ask(nc.vector.reduce_sum(st(2, ALLR), sqa, AX_X))
            link(ts(st(3, ALLR), st(3, ALLR), MIN_NORM, None, ALU.max))
            link(ts(st(11), st(10), ARTANH_CLIP, None, ALU.min))
            artanh(12, 11)
            link(nc.vector.reciprocal(st(4), st(10)))
            link(tt(st(4), st(4), st(3), ALU.mult))
            link(tt(st(8), st(4), st(12), ALU.mult))
            ask(nc.vector.tensor_copy(stat[A, 8, TILES:ALLR], stat[A, 3, TILES:ALLR]))
            link(ts(st(9, ALLR), st(9, ALLR), MAX_NORM, None, ALU.min))
            link(nc.vector.reciprocal(st(4, ALLR), st(3, ALLR)))
            link(tt(st(4, ALLR), st(4, ALLR), st(9, ALLR), ALU.mult))
            link(tt(mx, mx, wide(4, ALLR), ALU.mult))
            res, hyp_bias = work[0][A, 0:TILES, :], work[0][A, TILES:ALLR, :].to_broadcast([ROWS, TILES, D])
            link(tt(sqa, mx, mx, ALU.mult))
            link(nc.vector.reduce_sum(st(5, ALLR), sqa, AX_X))
            link(tt(sq, res, hyp_bias, ALU.mult))
            link(nc.vector.reduce_sum(st(6), sq, AX_X))
            y2 = stat[A, 5, TILES:ALLR]
            link(ts(st(6), st(6), 2.0, 1.0, ALU.mult, ALU.add))
            link(ts(st(7), st(6), y2, None, ALU.add))
            link(ts(st(8), st(5), y2, None, ALU.mult))
            link(tt(st(8), st(8), st(6), ALU.add))
            link(ts(st(8), st(8), MIN_NORM, None, ALU.max))
            link(nc.vector.reciprocal(st(8), st(8)))
            link(ts(st(9), st(5), -1.0, 1.0, ALU.mult, ALU.add))
            link(tt(st(7), st(7), st(8), ALU.mult))
            link(tt(st(9), st(9), st(8), ALU.mult))
            link(tt(sq, res, wide(7), ALU.mult))
            link(tt(h0, hyp_bias, wide(9), ALU.mult))
            link(tt(h0, h0, sq, ALU.add))
            link(tt(sq, h0, h0, ALU.mult))
            ask(nc.vector.reduce_sum(st(0), sq, AX_X))
            link(ts(st(10), st(1), MIN_NORM, None, ALU.max))
            link(ts(st(11), st(10), MAX_NORM, None, ALU.min))
            artanh(12, 11)
            link(nc.vector.reciprocal(st(4), st(10)))
            link(tt(st(4), st(4), st(12), ALU.mult))
            tt(h0, h0, wide(4), ALU.mult).then_inc(xt_ready, 1)

            dve.wait_ge(adj_loaded, 64)
            dve.wait_ge(ident_set, 3)
            nc.vector.tensor_reduce(adj_tile_max[A, :], adj[A, :, :].rearrange("p t n -> p n t"),
                                    AX_X, ALU.max).then_inc(tile_max_ready, 1)
            dve.wait_ge(tile_max_turned, 1)
            for b in range(3):
                k = min(QUARTER, TILES - QUARTER * b)
                ins = nc.vector.tensor_reduce(adj_row_max[A, QUARTER * b:QUARTER * b + k],
                                              t_ps[A, b, 0:k * D].rearrange("p (t m) -> p t m", m=D)[:, :, 0:ROWS],
                                              AX_X, ALU.max)
                if b < 2:
                    link(ins)
            ins.then_inc(row_max_ready, 1)

            dve.wait_ge(support_ready, 1)
            sup = work[0][A, 0:TILES, :]
            for b in range(3):
                k = min(QUARTER, TILES - QUARTER * b)
                link(nc.vector.tensor_copy(work[0][A, QUARTER * b:QUARTER * b + k, :],
                                           s_ps[A, b, 0:k * D].rearrange("p (t d) -> p t d", d=D)))
            link(tt(sq, sup, sup, ALU.mult))
            ask(nc.vector.reduce_sum(st(0), sq, AX_X))
            link(ts(st(1), st(1), MIN_NORM, None, ALU.max))
            link(nc.vector.reciprocal(st(2), st(1)))
            link(ts(st(1), st(1), ARTANH_MAX_NORM, None, ALU.min))
            link(tt(st(1), st(1), st(2), ALU.mult))
            link(stt(out=sup, in0=sup, scalar=0.0, in1=wide(1), op0=ALU.max, op1=ALU.mult))
            link(tt(sq, sup, sup, ALU.mult))
            ask(nc.vector.reduce_sum(st(0), sq, AX_X))
            ask(ts(st(2), st(1), MIN_NORM, None, ALU.max))
            link(ts(st(3), st(3), MAX_NORM, None, ALU.min))
            link(nc.vector.reciprocal(st(2), st(2)))
            link(tt(st(2), st(2), st(3), ALU.mult))
            link(tt(sup, sup, wide(2), ALU.mult))
            link(tt(x_rows[A], x_rows[A], sup, ALU.add))

            layernorm_relu(x_rows[A], h0, h0, sq).then_inc(rows_ready, 1)
            dve.wait_ge(rows_turned, 2)
            for b in range(3):
                k = min(QUARTER, TILES - QUARTER * b)
                ins = nc.vector.tensor_copy(rows_t[:, QUARTER * b:QUARTER * b + k, :],
                                            s_ps[:, b, 0:k * D].rearrange("p (t r) -> p t r", r=D)[:, :, 0:ROWS])
            ins.then_inc(rows_t_ready, 1)

            dve.wait_ge(row_max_loaded, 16)
            for t in range(TILES):
                g = [t >= t0 for t0, _ in GROUPS].count(True) - 1
                for c in range(4):
                    n = 6 * t + c
                    dve.wait_ge(high_done, n + 1)
                    cols = slice((t - GROUPS[g][0]) * D, (t - GROUPS[g][0] + 1) * D)
                    r = 4 * (c % 2)
                    tt(stage[g % 2][A, c // 2, H + r:H + r + 4, cols],
                       proj_bank[n % 7][A, :].rearrange("p (h j) -> p h j", j=D),
                       stage[g % 2][A, c // 2, r:r + 4, cols], ALU.subtract).then_inc(low_done, 1)
                tt(adj[A, t, 0:N], adj[A, t, 0:N], adj_max_b[A, :], ALU.subtract).then_inc(adj_shifted, 1)

            dve.wait_ge(pads_set, 1)
            dve.wait_ge(e_ready, TILES)

            def max_half(it, off, s, half):
                b = off % 2
                dve.wait_ge(scores_ready, head(it, off) * (2 * TILES) + 2 * s + half + 1)
                nc.vector.reduce_max(half_max[b][:, s, half:half + 1], s_slot[half][:, 0:HALF], AX_X).then_inc(scores_maxed, 1)

            def join_halves(it, off):
                b = off % 2
                dve.wait_ge(scores_maxed, head(it, off) * (2 * TILES) + 2 * TILES)
                if exists(it, off - 2):
                    dve.wait_ge(neg_max_placed[b], turn(it, off) * 32)
                nc.vector.tensor_reduce(neg_max[b][:], half_max[b][:], AX_X, ALU.max, negate=True).then_inc(neg_max_ready, 1)

            def product(it, off, t):
                dve.wait_ge(exp_done, head(it, off) * (3 * TILES) + 3 * (t + 1))
                nc.vector.tensor_tensor(probs[t][A, :], probs[t][A, :], adj[A, t, 0:N], ALU.mult).then_inc(vec_probs, 1)

            def max_tile(it, off, s):
                for half in range(2):
                    max_half(it, off, s, half)
                if s == TILES - 1:
                    join_halves(it, off)

            for u in range(TILES + LEAD):
                max_tile(0, u // TILES, u % TILES)

            def head_steps(it, off):
                for i in range(TILES):
                    ahead = off + 1 + (i + LEAD) // TILES
                    if exists(it, ahead):
                        max_tile(it, ahead, (i + LEAD) % TILES)
                    back = off if i else off - 1
                    if (i - 1) % TILES in VEC_TILES and exists(it, back):
                        product(it, back, (i - 1) % TILES)

            head_loop(dve, head_steps)
            if TILES - 1 in VEC_TILES:
                product(HEADS // 2 - 1, 1, TILES - 1)

            dve.wait_ge(o_loaded, 32)
            nc.vector.reciprocal(recip_sum[A, :], o_rows[A, H, :]).then_inc(recip_ready, 1)
            dve.wait_ge(recip_ready, 1)
            for h in range(6):
                tt(o_rows[A, h, :], o_rows[A, h, :], recip_sum[A, :], ALU.mult).then_inc(normed_v, 1)
            for t in range(TILES + 1):
                if t < TILES:
                    if t >= 2:
                        dve.wait_ge(y_ready, t - 1)
                    dve.wait_ge(o_turned, t + 1)
                    ins = nc.vector.tensor_copy(o_t[t % 2][:, :, 0:ROWS],
                                                s_slot[t % 2].rearrange("p (h r) -> p h r", r=D)[:, :, 0:ROWS])
                    ins.then_inc(o_t_ready, 1)
                if t >= 1:
                    dve.wait_ge(y_ready, t)
                    tt(y_rows[A, t - 1, :], x_rows[A, t - 1, :], t_ps[A, (t - 1) % 3, 0:D], ALU.add).then_inc(y_added, 1)

        @block.tensor
        def _(pe):
            mm = nc.tensor.matmul

            def turn_rows(n):
                pe.wait_ge(rows_ready, n)
                for t in range(TILES):
                    ins = nc.tensor.transpose(s_ps[:, t // QUARTER, (t % QUARTER) * D:(t % QUARTER) * D + ROWS],
                                              work[1][0:ROWS, t, :], ident[0:ROWS, 0:ROWS])
                ins.then_inc(rows_turned, 1)
                pe.wait_ge(rows_t_ready, n)

            pe.wait_ge(ident_set, 2)
            turn_rows(1)
            pe.wait_ge(w0_loaded, 32)
            for t in range(TILES):
                ins = mm(t_ps[0:ROWS, t // QUARTER, (t % QUARTER) * D:(t % QUARTER + 1) * D], rows_t[:, t, :], w0_sb[:],
                         start=True, stop=True)
            ins.then_inc(mx_ready, 1)
            pe.wait_ge(xt_ready, 1)
            pe.wait_ge(tile_max_ready, 1)
            for s in range(TILES):
                ins = nc.tensor.transpose(t_ps[0:ROWS, s // QUARTER, (s % QUARTER) * D:(s % QUARTER) * D + ROWS],
                                          adj_tile_max[0:ROWS, s::TILES], ident[0:ROWS, 0:ROWS])
            ins.then_inc(tile_max_turned, 1)
            pe.wait_ge(adj_loaded, 64)
            for s in range(TILES):
                for t in range(TILES):
                    k = ROWS if t == 0 else FULL
                    ins = mm(s_ps[0:ROWS, s // QUARTER, (s % QUARTER) * D:(s % QUARTER + 1) * D],
                             adj[0:k, t, s::TILES], work[1][0:k, t, :], start=t == 0, stop=t == TILES - 1)
            ins.then_inc(support_ready, 1)
            turn_rows(2)
            pe.wait_ge(row_max_ready, 1)
            pe.wait_ge(w_loaded, 48)
            n = 0
            for t in range(TILES):
                for c in range(6):
                    if n >= 7:
                        if (n - 7) % 6 < 4:
                            pe.wait_ge(low_done, (n - 7) // 6 * 4 + (n - 7) % 6 + 1)
                        else:
                            pe.wait_ge(high_done, n - 7 + 1)
                    w = wqk_sb[:, c * BANK:(c + 1) * BANK] if c < 4 else wv_sb[:, (c - 4) * BANK:(c - 3) * BANK]
                    mm(proj_bank[n % 7][0:ROWS, :], rows_t[:, t, :], w, start=True, stop=True).then_inc(proj_done, 1)
                    n += 1
            pe.wait_ge(low_done, 4 * TILES)
            pe.wait_ge(high_done, 6 * TILES)

            def score_half(it, off, s, half, static_first):
                b = off % 2
                if s == 0 and half == 0:
                    pe.wait_ge(max_ops_loaded[b], turn(it, off) * 96 + 96)
                if not static_first:
                    pe.wait_ge(scores_maxed, head(it, off) * (2 * TILES) + 2 * s + half - 1)
                q = q_max[b][:, s::TILES]
                mm(s_slot[half][:, 0:BANK], q, k_max[b][:, half * HALF:half * HALF + BANK], start=True, stop=True)
                mm(s_slot[half][:, BANK:HALF], q, k_max[b][:, half * HALF + BANK:(half + 1) * HALF],
                   start=True, stop=True).then_inc(scores_ready, 1)

            def shifted_third(it, off, t, c):
                b = off % 2
                if t == 0 and c == 0:
                    pe.wait_ge(exp_ops_loaded[b], turn(it, off) * 96 + 96)
                    pe.wait_ge(neg_max_placed[b], turn(it, off) * 32 + 32)
                if t > 0 or exists(it, off - 1):
                    pe.wait_ge(exp_done, head(it, off) * (3 * TILES) + 3 * t + c - 2)
                c0, w = EXP_COLS[c]
                mm(t_ps[:, c, 0:w], k_exp[b][:, t::TILES], q_exp[b][:, c0:c0 + w], start=True, stop=True).then_inc(shifted_ready, 1)

            def weighted_sum(it, off, t):
                b = off % 2
                if t == 0:
                    pe.wait_ge(v_loaded[b], turn(it, off) * 32 + 32)
                    if exists(it, off - 1):
                        pe.wait_ge(sums_copied, head(it, off))
                if t in VEC_TILES:
                    pe.wait_ge(vec_probs, head(it, off) * len(VEC_TILES) + VEC_TILES.index(t) + 1)
                else:
                    pe.wait_ge(pool_probs, head(it, off) * len(POOL_TILES) + POOL_TILES.index(t) + 1)
                for c, (c0, w) in enumerate(SUM_COLS):
                    ins = mm(o_ps[32 * c:32 * c + VROW, 0:w], v_sb[b][0:ROWS, t * VROW:(t + 1) * VROW],
                             probs[t][0:ROWS, c0:c0 + w], start=t == 0, stop=t == TILES - 1)
                ins.then_inc(tile_summed, 1)

            for u in range(TILES + LEAD):
                for half in range(2):
                    score_half(0, u // TILES, u % TILES, half, u == 0)

            def head_steps(it, off):
                for i in range(TILES):
                    ahead, s = off + 1 + (i + LEAD) // TILES, (i + LEAD) % TILES
                    if exists(it, ahead):
                        score_half(it, ahead, s, 0, False)
                    shifted_third(it, off, i, 0)
                    shifted_third(it, off, i, 1)
                    if exists(it, ahead):
                        score_half(it, ahead, s, 1, False)
                    shifted_third(it, off, i, 2)
                    back = off if i >= LAG else off - 1
                    if exists(it, back):
                        weighted_sum(it, back, (i - LAG) % TILES)

            head_loop(pe, head_steps)
            for t in range(TILES - LAG, TILES):
                weighted_sum(HEADS // 2 - 1, 1, t)

            pe.wait_ge(normed_v, 6)
            pe.wait_ge(normed_p, 2)
            for t in range(TILES + 1):
                if t < TILES:
                    if t >= 2:
                        pe.wait_ge(o_t_ready, t - 1)
                    for h in range(H):
                        ins = nc.tensor.transpose(s_slot[t % 2][:, h * D:h * D + ROWS],
                                                  o_rows[0:ROWS, h, t * D:(t + 1) * D], ident[0:ROWS, 0:ROWS])
                    ins.then_inc(o_turned, 1)
                if t >= 1:
                    pe.wait_ge(o_t_ready, t)
                    if t >= 4:
                        pe.wait_ge(y_added, t - 3)
                    for h in range(H):
                        ins = mm(t_ps[0:ROWS, (t - 1) % 3, 0:D], o_t[(t - 1) % 2][:, h, 0:ROWS], wo_sb[:, h * D:(h + 1) * D],
                                 start=h == 0, stop=h == H - 1)
                    ins.then_inc(y_ready, 1)


def kernel(x, adj, L0_gnn_weight, L0_gnn_bias, L1_gnn_Wq, L1_gnn_Wk, L1_gnn_Wv, L1_gnn_Wo):
    import numpy as np
    import concourse.bacc as bacc
    from concourse.bass_utils import run_bass_kernel_spmd

    def by_head(w):
        return np.asarray(w).reshape(D, H, D).transpose(2, 1, 0).reshape(D, C)

    arrays = {
        "x": np.asarray(x),
        "adj_t": np.asarray(adj).T,
        "w0_t": np.asarray(L0_gnn_weight).T,
        "bias": np.asarray(L0_gnn_bias).reshape(1, D),
        "wqk": np.concatenate([by_head(L1_gnn_Wq), by_head(L1_gnn_Wk)], axis=1),
        "wv": np.asarray(L1_gnn_Wv).T,
        "wo": np.asarray(L1_gnn_Wo).reshape(D, D, H).transpose(1, 2, 0).reshape(D, H * D),
    }
    arrays = {f"in_{n}": np.ascontiguousarray(a) for n, a in arrays.items()}
    nc = bacc.Bacc("TRN2", target_bir_lowering=False, num_devices=1)
    args = [nc.dram_tensor(n, a.shape, F32, kind="ExternalInput").ap() for n, a in arrays.items()]
    out = nc.dram_tensor("out", (N, D), F32, kind="ExternalOutput").ap()
    build_block(nc, *args, out)
    result = run_bass_kernel_spmd(nc, [arrays], core_ids=[0])
    return result.results[0]["out"]
```

```python
import concourse.bass as bass
from concourse import mybir
from contextlib import ExitStack

F32 = mybir.dt.float32
F16 = mybir.dt.float16
ALU = mybir.AluOpType
ACT = mybir.ActivationFunctionType
AX_X = mybir.AxisListType.X

N, D, H = 1354, 128, 8
P = 128
C = D * H
HEADS = D
FLAT = N * D
TILES = -(-N // P)
FULL = N // TILES
ROWS = FULL + 1
LASTROW = FULL * TILES
PADN = TILES * P
ADJW = TILES * ROWS
LN_EPS = 1e-5
MIN_NORM = 1e-15
MAX_NORM = 1.0 - 0.004
ARTANH_CLIP = 1.0 - 2.0 ** -23
ARTANH_MAX_NORM = 3.1063029
SCALE = float(D) ** -0.5

HALF = N // 2
BANK = 512
PEW = 160
POOLW = 860
EDGES = (0, 512, PEW + POOLW, N)
EXP_COLS = [(a, b - a) for a, b in zip(EDGES, EDGES[1:])]
SUMW = 339
SUM_COLS = [(c * SUMW, min(SUMW, N - c * SUMW)) for c in range(4)]
VROW = H + 1
LEAD = 3
LAG = 4
BLOCKS = [(r, min(P, N - r)) for r in range(0, N, P)]
STAGES = 5
V_STAGES = 3
FIRST_MAX = 3
EARLY = (HEADS - 2) * N // PADN
STAGED_FROM = (TILES * N - 3 * 2 * C) // N
QUARTER = BANK // D


def build_block(nc, x, adj_t, w0_t, bias, wqk, wv, wo, out):
    ctx = ExitStack()
    with ctx:
        def sb(name, shape, dt=F32):
            return ctx.enter_context(nc.sbuf_tensor(name, shape, dt))

        def ps(name, shape):
            return ctx.enter_context(nc.psum_tensor(name, shape, F32))

        def sem(name):
            return ctx.enter_context(nc.semaphore(name))

        q_split = nc.dram_tensor("q_split", (2 * H, FLAT), F16, kind="Internal").ap()
        k_split = nc.dram_tensor("k_split", (2 * H, FLAT), F16, kind="Internal").ap()
        v_rows = nc.dram_tensor("v_rows", (FLAT, VROW), F32, kind="Internal").ap()
        o_cols = nc.dram_tensor("o_cols", (VROW, FLAT), F32, kind="Internal").ap()
        adj_max_row = nc.dram_tensor("adj_max_row", (1, N), F32, kind="Internal").ap()

        adj_sb = sb("adj_sb", [P, TILES * ADJW])
        adj = adj_sb[:].rearrange("p (t n) -> p t n", t=TILES)
        ring = sb("ring", [P, TILES * N])
        probs = [ring[:, t * N:(t + 1) * N] for t in range(TILES)]
        rows_x = sb("rows_x", [P, TILES * D])
        shared = sb("shared", [P, VROW * PADN])
        wqk_sb, wv_sb = shared[:, 0:2 * C], shared[:, 2 * C:3 * C]
        row_t = shared[:, 3 * C:3 * C + ADJW]
        v_stage = shared[:, 4448:4448 + V_STAGES * D * VROW].rearrange("p (b c) -> p b c", b=V_STAGES)
        o_rows = shared[:].rearrange("p (h c) -> p h c", h=VROW)
        x_rows = rows_x[:].rearrange("p (t d) -> p t d", t=TILES)
        rows_t = row_t.rearrange("p (t r) -> p t r", t=TILES)
        rows_in_order = row_t.rearrange("p (r t) -> p t r", t=TILES)
        work = [ring[:, i * 1536:(i + 1) * 1536].rearrange("p (t d) -> p t d", d=D) for i in range(3)]
        adj_max_b = ring[:, 4608:4608 + N]
        adj_tile_max = ring[:, 6144:6144 + ADJW]
        w0_sb = ring[:, 7552:7552 + D]
        adj_part = ring[:, 7680:7680 + PEW]
        stage_words = 2 * C
        stage_at = [shared[:, VROW * PADN - stage_words:VROW * PADN],
                    *[ring[:, TILES * N - b * stage_words:TILES * N - (b - 1) * stage_words] for b in (1, 2, 3)],
                    shared[:, VROW * PADN - 2 * stage_words:VROW * PADN - stage_words]]
        stage = [s.bitcast(F16).rearrange("p (w r c) -> p w r c", w=2, r=2 * H) for s in stage_at]
        stat = sb("stat", [P, 13, TILES + 1])
        adj_parts = [adj[:, t, 0:PEW].bitcast(F16).rearrange("p (a n) -> p a n", a=2) for t in range(TILES)]
        ident_h = sb("ident_h", [P, P], F16)
        adj_row_max = sb("adj_row_max", [P, TILES])
        wo_sb = sb("wo_sb", [P, H * D])
        ident = sb("ident", [P, P])
        q_max = [sb(f"q_max{b}", [P, PADN], F16) for b in range(2)]
        k_max = [sb(f"k_max{b}", [P, PADN], F16) for b in range(2)]
        q_exp = [sb(f"q_exp{b}", [P, PADN], F16) for b in range(2)]
        k_exp = [sb(f"k_exp{b}", [P, PADN], F16) for b in range(2)]
        v_sb = [sb(f"v_sb{b}", [P, TILES * VROW]) for b in range(2)]
        half_max = [sb(f"half_max{b}", [P, TILES, 2]) for b in range(2)]
        neg_max = [sb(f"neg_max{b}", [P, TILES], F16) for b in range(2)]
        o_sb = [sb(f"o_sb{b}", [P, SUMW]) for b in range(2)]
        o_t = [ring[:, b * 1024:(b + 1) * 1024].rearrange("p (h r) -> p h r", h=H) for b in range(2)]
        recip_sum = ring[:, 2048:2048 + PADN]
        y_rows = ring[:, 4096:4096 + PADN].rearrange("p (t d) -> p t d", t=TILES)

        s_ps = ps("s_ps", [P, 4, BANK])
        t_ps = ps("t_ps", [P, 3, BANK])
        o_ps = ps("o_ps", [P, BANK])
        s_slot = [s_ps[:, 2 * b:2 * b + 2, :].rearrange("p b c -> p (b c)") for b in range(2)]
        proj_bank = [t_ps[:, b, :] for b in range(3)] + [o_ps[:]]

        x_loaded, w0_loaded, w_loaded, adj_loaded = sem("x_loaded"), sem("w0_loaded"), sem("w_loaded"), sem("adj_loaded")
        ident_set, pads_zeroed, pads_set = sem("ident_set"), sem("pads_zeroed"), sem("pads_set")
        dve_step, pool_step = sem("dve_step"), sem("pool_step")
        stat_ready, stat_done = sem("stat_ready"), sem("stat_done")
        rows_ready, rows_turned, rows_t_ready = sem("rows_ready"), sem("rows_turned"), sem("rows_t_ready")
        mx_ready, xt_ready, support_ready = sem("mx_ready"), sem("xt_ready"), sem("support_ready")
        tile_max_ready, tile_max_turned, row_max_ready = sem("tile_max_ready"), sem("tile_max_turned"), sem("row_max_ready")
        row_max_stored, row_max_loaded = sem("row_max_stored"), sem("row_max_loaded")
        adj_shifted, e_ready = sem("adj_shifted"), sem("e_ready")
        proj_done, high_done, low_done = sem("proj_done"), sem("high_done"), sem("low_done")
        qk_stored = [sem(f"qk_stored{b}") for b in range(STAGES)]
        v_stored = [sem(f"v_stored{b}") for b in range(V_STAGES)]
        max_ops_loaded = [sem(f"max_ops_loaded{b}") for b in range(2)]
        exp_ops_loaded = [sem(f"exp_ops_loaded{b}") for b in range(2)]
        v_loaded = [sem(f"v_loaded{b}") for b in range(2)]
        neg_max_placed = [sem(f"neg_max_placed{b}") for b in range(2)]
        scores_ready, scores_maxed = sem("scores_ready"), sem("scores_maxed")
        neg_max_ready = sem("neg_max_ready")
        shifted_ready, exp_done = sem("shifted_ready"), sem("exp_done")
        vec_probs, pool_probs = sem("vec_probs"), sem("pool_probs")
        tile_summed, sums_copied = sem("tile_summed"), sem("sums_copied")
        sums_stored = [sem(f"sums_stored{b}") for b in range(2)]
        o_early, o_loaded, recip_ready, normed_v, normed_p = sem("o_early"), sem("o_loaded"), sem("recip_ready"), sem("normed_v"), sem("normed_p")
        o_turned, o_t_low, o_t_high, y_ready, y_added, out_stored = sem("o_turned"), sem("o_t_low"), sem("o_t_high"), sem("y_ready"), sem("y_added"), sem("out_stored")

        block = ctx.enter_context(nc.Block())

        def head_loop(eng, steps):
            for off in range(2):
                steps(0, off)
            with eng.Fori(1, HEADS // 2 - 1) as it:
                for off in range(2):
                    steps(it, off)
            for off in range(2):
                steps(HEADS // 2 - 1, off)

        def exists(it, off):
            return not isinstance(it, int) or 0 <= 2 * it + off < HEADS

        def head(it, off):
            return it * 2 + off

        def turn(it, off):
            return it + off // 2

        def flat_tiles(arr):
            return arr[:, 0:LASTROW * D].rearrange("r (p c) -> p r c", c=TILES * D)

        def first_maxima(block_number):
            u = 2 * (block_number - FIRST_MAX)
            return [v for v in (u, u + 1) if 0 <= v < TILES + LEAD]

        @block.sync
        def _(sp):
            sp.dma_start(x_rows[0:FULL, :, :], x[0:LASTROW, :].rearrange("(p t) d -> p t d", t=TILES)).then_inc(x_loaded, 16)
            sp.dma_start(x_rows[FULL:ROWS, :, :],
                         x[LASTROW:N, :].unsqueeze(1).to_broadcast([1, TILES, D])).then_inc(x_loaded, 16)
            sp.dma_start(w0_sb, w0_t).then_inc(w0_loaded, 16)
            sp.dma_start(work[0][0:ROWS, TILES, :], bias.to_broadcast([ROWS, D])).then_inc(w0_loaded, 16)
            for t0, t1 in ((0, 4), (4, 8), (8, TILES)):
                sp.dma_start(adj[0:FULL, t0:t1, 0:N],
                             adj_t[0:LASTROW, :].rearrange("(p t) n -> p t n", t=TILES)[:, t0:t1, :]).then_inc(adj_loaded, 16)
            sp.dma_start(adj[FULL:ROWS, :, 0:N],
                         adj_t[LASTROW:N, :].unsqueeze(1).to_broadcast([1, TILES, N])).then_inc(adj_loaded, 16)
            sp.dma_start(wqk_sb, wqk).then_inc(w_loaded, 16)
            sp.dma_start(wv_sb, wv).then_inc(w_loaded, 16)
            sp.dma_start(wo_sb[:], wo).then_inc(w_loaded, 16)

            sp.wait_ge(row_max_ready, 1)
            sp.dma_start(adj_max_row[0, 0:LASTROW].rearrange("(p t) -> p t", t=TILES), adj_row_max[0:FULL, :]).then_inc(row_max_stored, 16)
            sp.dma_start(adj_max_row[0:1, LASTROW:N], adj_row_max[FULL:ROWS, 0:1]).then_inc(row_max_stored, 16)
            sp.wait_ge(row_max_stored, 32)
            sp.dma_start(adj_max_b[0:ROWS, :], adj_max_row.to_broadcast([ROWS, N])).then_inc(row_max_loaded, 16)

            def load_operands(q_dst, k_dst, it, off, signal):
                cols = bass.ds(head(it, off) * N, N)
                for i in range(2):
                    sp.dma_start(q_dst[2 * H * i:2 * H * (i + 1), 0:N], q_split[:, cols]).then_inc(signal, 16)
                    for j in range(2):
                        r = 2 * H * i + H * j
                        sp.dma_start(k_dst[r:r + H, 0:N], k_split[H * i:H * (i + 1), cols]).then_inc(signal, 16)

            def load_v(it, off):
                b, first = off % 2, head(it, off) * N
                src = v_rows[bass.ds(first, LASTROW), :].rearrange("(p t) c -> p (t c)", t=TILES)
                sp.dma_start(v_sb[b][0:FULL, :], src).then_inc(v_loaded[b], 16)
                sp.dma_start(v_sb[b][FULL:ROWS, 0:VROW], v_rows[bass.ds(first + LASTROW, 1), :]).then_inc(v_loaded[b], 16)

            def place_neg_max(b):
                sp.dma_start(q_exp[b][4 * H:4 * H + 1, 0:LASTROW], neg_max[b][0:FULL, :]).then_inc(neg_max_placed[b], 16)
                sp.dma_start(q_exp[b][4 * H:4 * H + 1, LASTROW:N], neg_max[b][FULL:ROWS, 0:1]).then_inc(neg_max_placed[b], 16)

            def store_sums(it, off):
                b = off % 2
                for c, (c0, w) in enumerate(SUM_COLS):
                    sp.dma_start(o_cols[:, bass.ds(head(it, off) * N + c0, w)],
                                 o_sb[b][32 * c:32 * c + VROW, 0:w]).then_inc(sums_stored[b], 16)

            v_by_row = v_rows.rearrange("(r j) c -> r (j c)", j=D)
            for k, (r0, n) in enumerate(BLOCKS):
                sp.wait_ge(low_done, 4 * (k + 1))
                for w, arr in enumerate((q_split, k_split)):
                    sp.dma_start(arr[:, r0 * D:(r0 + n) * D].rearrange("r (p j) -> p r j", j=D),
                                 stage[k % STAGES][0:n, w, :, :]).then_inc(qk_stored[k % STAGES], 16)
                sp.wait_ge(high_done, 6 * (k + 1))
                sp.dma_start(v_by_row[r0:r0 + n, :], v_stage[0:n, k % V_STAGES, :]).then_inc(v_stored[k % V_STAGES], 16)
                if k == FIRST_MAX + 5:
                    sp.wait_ge(neg_max_ready, 1)
                    place_neg_max(0)
                if k == 1:
                    sp.wait_ge(qk_stored[0], 32)
                    sp.wait_ge(v_stored[0], 16)
                    sp.wait_ge(pads_set, 1)
                    for off in range(2):
                        load_operands(q_max[off], k_max[off], 0, off, max_ops_loaded[off])
                    load_operands(q_exp[0], k_exp[0], 0, 0, exp_ops_loaded[0])
                    load_v(0, 0)
            for b in range(STAGES):
                sp.wait_ge(qk_stored[b], 32 * len(BLOCKS[b::STAGES]))
            for b in range(V_STAGES):
                sp.wait_ge(v_stored[b], 16 * len(BLOCKS[b::V_STAGES]))

            def head_steps(it, off):
                b = off % 2
                if exists(it, off + 2):
                    sp.wait_ge(scores_ready, head(it, off) * (2 * TILES) + 2 * TILES)
                    load_operands(q_max[b], k_max[b], it, off + 2, max_ops_loaded[b])
                if exists(it, off + 1):
                    if exists(it, off - 1):
                        sp.wait_ge(shifted_ready, head(it, off) * (3 * TILES))
                    load_operands(q_exp[1 - b], k_exp[1 - b], it, off + 1, exp_ops_loaded[1 - b])
                    if exists(it, off - 1):
                        sp.wait_ge(tile_summed, head(it, off) * TILES)
                    load_v(it, off + 1)
                if exists(it, off - 1):
                    sp.wait_ge(sums_copied, head(it, off))
                    store_sums(it, off - 1)
                if exists(it, off + 1):
                    sp.wait_ge(neg_max_ready, head(it, off) + 2)
                    place_neg_max(1 - b)

            head_loop(sp, head_steps)
            sp.wait_ge(sums_copied, HEADS)
            store_sums(HEADS // 2 - 1, 1)
            for b in range(2):
                sp.wait_ge(sums_stored[b], 64 * (HEADS // 2))

            sp.dma_start(o_rows[EARLY:FULL, :, :], flat_tiles(o_cols)[EARLY:FULL, :, :]).then_inc(o_loaded, 16)
            last = o_cols[:, LASTROW * D:FLAT].unsqueeze(0).unsqueeze(2).to_broadcast([1, VROW, TILES, D])
            sp.dma_start(o_rows[FULL:ROWS, :, :].rearrange("p h (t c) -> p h t c", t=TILES), last).then_inc(o_loaded, 16)
            half = TILES // 2 + 2
            out_rows = out[0:LASTROW, :].rearrange("(p t) d -> p t d", t=TILES)
            sp.wait_ge(y_added, half)
            sp.dma_start(out_rows[:, 0:half, :], y_rows[0:FULL, 0:half, :]).then_inc(out_stored, 16)
            sp.dma_start(out[LASTROW:N, :], y_rows[FULL:ROWS, 0, :]).then_inc(out_stored, 16)
            sp.wait_ge(y_added, TILES)
            sp.dma_start(out_rows[:, half:TILES, :], y_rows[0:FULL, half:TILES, :]).then_inc(out_stored, 16)
            sp.wait_ge(out_stored, 48)

        @block.gpsimd
        def _(pool):
            nc.gpsimd.memset(ident[:], 0.0).then_inc(ident_set, 1)
            pool.wait_ge(ident_set, 1)
            nc.gpsimd.affine_select(out=ident[:], in_=ident[:], compare_op=ALU.not_equal, fill=1.0,
                                    base=0, pattern=[[-1, P]], channel_multiplier=1).then_inc(ident_set, 1)
            pool.wait_ge(ident_set, 2)
            nc.gpsimd.tensor_copy(ident_h[:], ident[:]).then_inc(ident_set, 1)
            nc.gpsimd.memset(adj[:, :, N:ADJW], 0.0).then_inc(ident_set, 1)
            nc.gpsimd.memset(v_stage, 1.0).then_inc(ident_set, 1)
            for b in range(2):
                for buf in (q_max[b], k_max[b], q_exp[b], k_exp[b], v_sb[b], half_max[b]):
                    nc.gpsimd.memset(buf[:], 0.0).then_inc(pads_zeroed, 1)
            pool.wait_ge(pads_zeroed, 12)
            nc.gpsimd.memset(k_exp[0][4 * H:4 * H + 1, 0:N], 1.0).then_inc(pads_zeroed, 1)
            pool.wait_ge(pads_zeroed, 13)
            nc.gpsimd.memset(k_exp[1][4 * H:4 * H + 1, 0:N], 1.0).then_inc(pads_set, 1)

            links = [0]

            def link(ins):
                links[0] += 1
                ins.then_inc(pool_step, 1)
                pool.wait_ge(pool_step, links[0])

            tt = nc.gpsimd.tensor_tensor
            A = slice(0, ROWS)
            pool.wait_ge(pads_set, 1)
            pool.wait_ge(row_max_loaded, 16)
            pool.wait_ge(support_ready, 1)
            for t in range(TILES):
                high, low = adj_parts[t][A, 0, :], adj_parts[t][A, 1, :]
                link(tt(adj_part[A, :], adj[A, t, 0:PEW], adj_max_b[A, 0:PEW], ALU.subtract))
                link(nc.gpsimd.tensor_scalar(adj_part[A, :], adj_part[A, :], 2.0 / SCALE, None, ALU.mult))
                link(nc.gpsimd.tensor_copy(high, adj_part[A, :]))
                link(tt(low, adj_part[A, :], high, ALU.subtract))
                tt(adj[A, t, PEW:N], adj[A, t, PEW:N], adj_max_b[A, PEW:N], ALU.subtract).then_inc(adj_shifted, 1)
            pool.wait_ge(e_ready, TILES)

            def head_steps(it, off):
                for t in range(TILES):
                    pool.wait_ge(exp_done, head(it, off) * (3 * TILES) + 3 * t + 2)
                    cols = slice(PEW, PEW + POOLW)
                    nc.gpsimd.tensor_tensor(probs[t][0:ROWS, cols], probs[t][0:ROWS, cols], adj[0:ROWS, t, cols],
                                            ALU.mult).then_inc(pool_probs, 1)

            head_loop(pool, head_steps)
            for t in range(TILES):
                pool.wait_ge(recip_ready, t + 1)
                part = o_rows[A, H // 2:H, t * D:(t + 1) * D]
                tt(part, part, recip_sum[A, t * D:(t + 1) * D].unsqueeze(1).to_broadcast([ROWS, H // 2, D]),
                   ALU.mult).then_inc(normed_p, 1)

        @block.scalar
        def _(act):
            def row_stat(n, dst, src, func, **more):
                act.wait_ge(stat_ready, n)
                nc.scalar.activation(dst, src, func, **more).then_inc(stat_done, 1)

            A = slice(0, ROWS)
            row_stat(1, stat[A, 2, 0:TILES], stat[A, 1, 0:TILES], ACT.Sqrt)
            row_stat(2, stat[A, 1, 0:TILES], stat[A, 0, 0:TILES], ACT.Sqrt)
            row_stat(3, stat[A, 3, :], stat[A, 2, :], ACT.Sqrt)
            row_stat(4, stat[A, 8, 0:TILES], stat[A, 7, 0:TILES], ACT.Ln)
            row_stat(5, stat[A, 9, :], stat[A, 8, :], ACT.Tanh)
            row_stat(6, stat[A, 1, 0:TILES], stat[A, 0, 0:TILES], ACT.Sqrt)
            row_stat(7, stat[A, 8, 0:TILES], stat[A, 7, 0:TILES], ACT.Ln)
            row_stat(8, stat[A, 1, 0:TILES], stat[A, 0, 0:TILES], ACT.Sqrt)
            row_stat(9, stat[A, 1, 0:TILES], stat[A, 0, 0:TILES], ACT.Sqrt)
            row_stat(10, stat[A, 3, 0:TILES], stat[A, 2, 0:TILES], ACT.Tanh)
            row_stat(11, stat[A, 2, 0:TILES], stat[A, 1, 0:TILES], ACT.Sqrt)

            act.wait_ge(ident_set, 5)
            c_all = 0
            for k, (r0, n) in enumerate(BLOCKS):
                if k >= STAGES:
                    act.wait_ge(qk_stored[k % STAGES], 32 * (k // STAGES))
                if k >= V_STAGES:
                    act.wait_ge(v_stored[k % V_STAGES], 16 * (k // V_STAGES))
                for c in range(6):
                    act.wait_ge(proj_done, c_all + 1)
                    src = proj_bank[c_all % 4][0:n, :]
                    if c < 4:
                        dst = stage[k % STAGES][0:n, c // 2, 4 * (c % 2):4 * (c % 2) + 4, :]
                        src = src.rearrange("p (h j) -> p h j", j=D)
                    else:
                        dst = v_stage[0:n, k % V_STAGES, (c - 4) * 64 * VROW:(c - 3) * 64 * VROW].rearrange("p (j k) -> p j k", k=VROW)[:, :, 0:H]
                        src = src.rearrange("p (j k) -> p j k", k=H)
                    nc.scalar.activation(dst, src, ACT.Copy).then_inc(high_done, 1)
                    c_all += 1
                act.wait_ge(adj_shifted, k + 1)
                nc.scalar.activation(adj[A, k, PEW:N], adj[A, k, PEW:N], ACT.Exp, scale=2.0).then_inc(e_ready, 1)

            def head_steps(it, off):
                b = off % 2
                for i in range(TILES):
                    if isinstance(it, int) and it == off == 0 and i == STAGED_FROM:
                        for b in range(STAGES):
                            act.wait_ge(qk_stored[b], 32 * len(BLOCKS[b::STAGES]))
                    if exists(it, off - 1):
                        act.wait_ge(tile_summed, head(it, off) * TILES + (i + 1 - TILES))
                    for c, (c0, w) in enumerate(EXP_COLS):
                        act.wait_ge(shifted_ready, head(it, off) * (3 * TILES) + 3 * i + c + 1)
                        dst = t_ps[A, c, 0:w] if c == 2 else probs[i][A, c0:c0 + w]
                        nc.scalar.activation(dst, t_ps[A, c, 0:w], ACT.Exp, scale=SCALE).then_inc(exp_done, 1)
                        if i == LAG and c == 0 and exists(it, off - 1):
                            copy_sums(it, off - 1)
                    if not exists(it, off + 1) and i == 1:
                        bring_back_sums()

            def copy_sums(it, off):
                b = off % 2
                act.wait_ge(tile_summed, head(it, off) * TILES + TILES)
                if exists(it, off - 2):
                    act.wait_ge(sums_stored[b], turn(it, off) * 64)
                nc.scalar.activation(o_sb[b][:], o_ps[:, 0:SUMW], ACT.Copy).then_inc(sums_copied, 1)

            def bring_back_sums():
                for b in range(2):
                    act.wait_ge(sums_stored[b], 64 * (HEADS // 2 - 1))
                for h in range(VROW):
                    act.dma_start(o_rows[0:EARLY, h, :], flat_tiles(o_cols)[0:EARLY, h, :]).then_inc(o_early, 16)

            head_loop(act, head_steps)
            copy_sums(HEADS // 2 - 1, 1)
            for t in range(TILES):
                act.wait_ge(o_turned, t + 1)
                if t >= 2:
                    act.wait_ge(y_ready, t - 1)
                nc.scalar.activation(o_t[t % 2][:, 0:4, 0:ROWS], s_ps[:, 2 * (t % 2), :].rearrange("p (h r) -> p h r", r=D)[:, :, 0:ROWS],
                                     ACT.Copy).then_inc(o_t_low, 1)

        @block.vector
        def _(dve):
            steps = [0]
            asked = [0]

            def link(ins):
                steps[0] += 1
                ins.then_inc(dve_step, 1)
                dve.wait_ge(dve_step, steps[0])

            def ask(ins):
                asked[0] += 1
                ins.then_inc(stat_ready, 1)
                dve.wait_ge(stat_done, asked[0])

            A = slice(0, ROWS)
            tt, ts, stt = nc.vector.tensor_tensor, nc.vector.tensor_scalar, nc.vector.scalar_tensor_tensor

            def st(i, n=TILES):
                return stat[A, i, 0:n]

            def wide(i, n=TILES):
                return st(i, n).unsqueeze(2).to_broadcast([ROWS, n, D])

            def layernorm_relu(src, dst, centred, square):
                link(nc.vector.reduce_sum(st(0), src, AX_X))
                link(ts(st(0), st(0), -1.0 / D, None, ALU.mult))
                link(tt(centred, src, wide(0), ALU.add))
                link(tt(square, centred, centred, ALU.mult))
                link(nc.vector.reduce_sum(st(1), square, AX_X))
                ask(ts(st(1), st(1), 1.0 / D, LN_EPS, ALU.mult, ALU.add))
                link(nc.vector.reciprocal(st(2), st(2)))
                return stt(out=dst, in0=centred, scalar=0.0, in1=wide(2), op0=ALU.max, op1=ALU.mult)

            def artanh(dst, z):
                link(ts(st(4), st(z), 1.0, None, ALU.add))
                link(ts(st(5), st(z), -1.0, 1.0, ALU.mult, ALU.add))
                link(nc.vector.reciprocal(st(6), st(5)))
                ask(tt(st(7), st(4), st(6), ALU.mult))
                link(tt(st(4), st(z), st(z), ALU.mult))
                link(ts(st(5), st(4), 1.0 / 7, 1.0 / 5, ALU.mult, ALU.add))
                link(tt(st(5), st(5), st(4), ALU.mult))
                link(ts(st(5), st(5), 1.0 / 3, None, ALU.add))
                link(tt(st(5), st(5), st(4), ALU.mult))
                link(ts(st(5), st(5), 1.0, None, ALU.add))
                link(tt(st(5), st(5), st(z), ALU.mult))
                link(ts(st(8), st(8), 0.5, None, ALU.mult))
                link(ts(st(6), st(z), 0.1, None, ALU.is_lt))
                link(tt(st(5), st(5), st(8), ALU.subtract))
                link(tt(st(5), st(5), st(6), ALU.mult))
                link(tt(st(dst), st(8), st(5), ALU.add))

            dve.wait_ge(x_loaded, 32)
            h0 = work[1][A, 0:TILES, :]
            sq = work[2][A, 0:TILES, :]
            layernorm_relu(x_rows[A], h0, h0, sq).then_inc(rows_ready, 1)
            dve.wait_ge(rows_ready, 1)
            link(tt(sq, h0, h0, ALU.mult))
            ask(nc.vector.reduce_sum(st(0), sq, AX_X))
            link(ts(st(10), st(1), MIN_NORM, None, ALU.max))
            dve.wait_ge(rows_turned, 1)
            for b in range(3):
                k = min(QUARTER, TILES - QUARTER * b)
                ins = nc.vector.tensor_copy(rows_t[:, QUARTER * b:QUARTER * b + k, :],
                                            s_ps[:, b, 0:k * D].rearrange("p (t r) -> p t r", r=D)[:, :, 0:ROWS])
            ins.then_inc(rows_t_ready, 1)

            dve.wait_ge(w0_loaded, 32)
            dve.wait_ge(mx_ready, 1)
            for b in range(3):
                k = min(QUARTER, TILES - QUARTER * b)
                link(nc.vector.tensor_copy(work[0][A, QUARTER * b:QUARTER * b + k, :],
                                           t_ps[A, b, 0:k * D].rearrange("p (t d) -> p t d", d=D)))
            ALLR = TILES + 1
            mx = work[0][A, 0:ALLR, :]
            sqa = work[2][A, 0:ALLR, :]
            link(tt(sqa, mx, mx, ALU.mult))
            ask(nc.vector.reduce_sum(st(2, ALLR), sqa, AX_X))
            link(ts(st(3, ALLR), st(3, ALLR), MIN_NORM, None, ALU.max))
            link(ts(st(11), st(10), ARTANH_CLIP, None, ALU.min))
            artanh(12, 11)
            link(nc.vector.reciprocal(st(4), st(10)))
            link(tt(st(4), st(4), st(3), ALU.mult))
            link(tt(st(8), st(4), st(12), ALU.mult))
            ask(nc.vector.tensor_copy(stat[A, 8, TILES:ALLR], stat[A, 3, TILES:ALLR]))
            link(ts(st(9, ALLR), st(9, ALLR), MAX_NORM, None, ALU.min))
            link(nc.vector.reciprocal(st(4, ALLR), st(3, ALLR)))
            link(tt(st(4, ALLR), st(4, ALLR), st(9, ALLR), ALU.mult))
            link(tt(mx, mx, wide(4, ALLR), ALU.mult))
            res, hyp_bias = work[0][A, 0:TILES, :], work[0][A, TILES:ALLR, :].to_broadcast([ROWS, TILES, D])
            link(tt(sqa, mx, mx, ALU.mult))
            link(nc.vector.reduce_sum(st(5, ALLR), sqa, AX_X))
            link(tt(sq, res, hyp_bias, ALU.mult))
            link(nc.vector.reduce_sum(st(6), sq, AX_X))
            y2 = stat[A, 5, TILES:ALLR]
            link(ts(st(6), st(6), 2.0, 1.0, ALU.mult, ALU.add))
            link(ts(st(7), st(6), y2, None, ALU.add))
            link(ts(st(8), st(5), y2, None, ALU.mult))
            link(tt(st(8), st(8), st(6), ALU.add))
            link(ts(st(8), st(8), MIN_NORM, None, ALU.max))
            link(nc.vector.reciprocal(st(8), st(8)))
            link(ts(st(9), st(5), -1.0, 1.0, ALU.mult, ALU.add))
            link(tt(st(7), st(7), st(8), ALU.mult))
            link(tt(st(9), st(9), st(8), ALU.mult))
            link(tt(sq, res, wide(7), ALU.mult))
            link(tt(h0, hyp_bias, wide(9), ALU.mult))
            link(tt(h0, h0, sq, ALU.add))
            link(tt(sq, h0, h0, ALU.mult))
            ask(nc.vector.reduce_sum(st(0), sq, AX_X))
            link(ts(st(10), st(1), MIN_NORM, None, ALU.max))
            link(ts(st(11), st(10), MAX_NORM, None, ALU.min))
            artanh(12, 11)
            link(nc.vector.reciprocal(st(4), st(10)))
            link(tt(st(4), st(4), st(12), ALU.mult))
            tt(h0, h0, wide(4), ALU.mult).then_inc(xt_ready, 1)

            dve.wait_ge(adj_loaded, 64)
            dve.wait_ge(ident_set, 4)
            nc.vector.tensor_reduce(adj_tile_max[A, :], adj[A, :, :].rearrange("p t n -> p n t"),
                                    AX_X, ALU.max).then_inc(tile_max_ready, 1)
            dve.wait_ge(tile_max_turned, 1)
            for b in range(3):
                k = min(QUARTER, TILES - QUARTER * b)
                ins = nc.vector.tensor_reduce(adj_row_max[A, QUARTER * b:QUARTER * b + k],
                                              t_ps[A, b, 0:k * D].rearrange("p (t m) -> p t m", m=D)[:, :, 0:ROWS],
                                              AX_X, ALU.max)
                if b < 2:
                    link(ins)
            ins.then_inc(row_max_ready, 1)

            dve.wait_ge(support_ready, 1)
            sup = work[0][A, 0:TILES, :]
            for b in range(3):
                k = min(QUARTER, TILES - QUARTER * b)
                link(nc.vector.tensor_copy(work[0][A, QUARTER * b:QUARTER * b + k, :],
                                           s_ps[A, b, 0:k * D].rearrange("p (t d) -> p t d", d=D)))
            link(tt(sq, sup, sup, ALU.mult))
            ask(nc.vector.reduce_sum(st(0), sq, AX_X))
            link(ts(st(1), st(1), MIN_NORM, None, ALU.max))
            link(nc.vector.reciprocal(st(2), st(1)))
            link(ts(st(1), st(1), ARTANH_MAX_NORM, None, ALU.min))
            link(tt(st(1), st(1), st(2), ALU.mult))
            link(stt(out=sup, in0=sup, scalar=0.0, in1=wide(1), op0=ALU.max, op1=ALU.mult))
            link(tt(sq, sup, sup, ALU.mult))
            ask(nc.vector.reduce_sum(st(0), sq, AX_X))
            ask(ts(st(2), st(1), MIN_NORM, None, ALU.max))
            link(ts(st(3), st(3), MAX_NORM, None, ALU.min))
            link(nc.vector.reciprocal(st(2), st(2)))
            link(tt(st(2), st(2), st(3), ALU.mult))
            link(tt(sup, sup, wide(2), ALU.mult))
            link(tt(x_rows[A], x_rows[A], sup, ALU.add))

            layernorm_relu(x_rows[A], h0, h0, sq).then_inc(rows_ready, 1)
            dve.wait_ge(rows_turned, 2)
            for b in range(3):
                k = min(QUARTER, TILES - QUARTER * b)
                ins = nc.vector.tensor_copy(rows_in_order[:, QUARTER * b:QUARTER * b + k, :],
                                            s_ps[:, b, 0:k * D].rearrange("p (t r) -> p t r", r=D)[:, :, 0:ROWS])
            ins.then_inc(rows_t_ready, 1)

            def max_half(it, off, s, half):
                b = off % 2
                dve.wait_ge(scores_ready, head(it, off) * (2 * TILES) + 2 * s + half + 1)
                nc.vector.reduce_max(half_max[b][:, s, half:half + 1], s_slot[half][:, 0:HALF], AX_X).then_inc(scores_maxed, 1)

            def join_halves(it, off):
                b = off % 2
                dve.wait_ge(scores_maxed, head(it, off) * (2 * TILES) + 2 * TILES)
                if exists(it, off - 2):
                    dve.wait_ge(neg_max_placed[b], turn(it, off) * 32)
                nc.vector.tensor_reduce(neg_max[b][:], half_max[b][:], AX_X, ALU.max, negate=True).then_inc(neg_max_ready, 1)

            def product(it, off, t):
                if exists(it, off - 1):
                    dve.wait_ge(tile_summed, head(it, off) * TILES + (t + 1 - TILES))
                dve.wait_ge(exp_done, head(it, off) * (3 * TILES) + 3 * (t + 1))
                c0, w = EXP_COLS[2]
                nc.vector.tensor_tensor(probs[t][A, c0:c0 + w], t_ps[A, 2, 0:w], adj[A, t, c0:c0 + w],
                                        ALU.mult).then_inc(vec_probs, 1)

            for k, (r0, n) in enumerate(BLOCKS):
                tiles = first_maxima(k)

                def low(c):
                    c_all = 6 * k + c
                    dve.wait_ge(high_done, c_all + 1)
                    r = 4 * (c % 2)
                    tt(stage[k % STAGES][0:n, c // 2, H + r:H + r + 4, :],
                       proj_bank[c_all % 4][0:n, :].rearrange("p (h j) -> p h j", j=D),
                       stage[k % STAGES][0:n, c // 2, r:r + 4, :], ALU.subtract).then_inc(low_done, 1)

                def maximum(i, half):
                    if i < len(tiles):
                        if tiles[i] == 0 and half == 0:
                            dve.wait_ge(pads_set, 1)
                        max_half(0, tiles[i] // TILES, tiles[i] % TILES, half)
                        if tiles[i] % TILES == TILES - 1 and half == 1:
                            join_halves(0, 0)

                low(0)
                low(1)
                maximum(0, 0)
                low(2)
                low(3)
                maximum(0, 1)
                maximum(1, 0)
                maximum(1, 1)
            dve.wait_ge(e_ready, TILES)

            def head_steps(it, off):
                for i in range(TILES):
                    ahead, s = off + 1 + (i + LEAD) // TILES, (i + LEAD) % TILES
                    for half in range(2):
                        if exists(it, ahead):
                            max_half(it, ahead, s, half)
                    product(it, off, i)
                    if s == TILES - 1 and exists(it, ahead):
                        join_halves(it, ahead)

            head_loop(dve, head_steps)

            dve.wait_ge(o_early, 16 * VROW)
            dve.wait_ge(o_loaded, 32)

            def normalise(t):
                cols = slice(t * D, (t + 1) * D)
                nc.vector.reciprocal(recip_sum[A, cols], o_rows[A, H, cols]).then_inc(recip_ready, 1)
                dve.wait_ge(recip_ready, t + 1)
                part = o_rows[A, 0:H // 2, cols]
                tt(part, part, recip_sum[A, cols].unsqueeze(1).to_broadcast([ROWS, H // 2, D]), ALU.mult).then_inc(normed_v, 1)

            normalise(0)
            normalise(1)
            for t in range(TILES + 1):
                if t < TILES:
                    if t >= 2:
                        dve.wait_ge(y_ready, t - 1)
                    dve.wait_ge(o_turned, t + 1)
                    nc.vector.tensor_copy(o_t[t % 2][:, 4:8, 0:ROWS],
                                          s_ps[:, 2 * (t % 2) + 1, :].rearrange("p (h r) -> p h r", r=D)[:, :, 0:ROWS]).then_inc(o_t_high, 1)
                    if t + 2 < TILES:
                        normalise(t + 2)
                if t >= 1:
                    dve.wait_ge(y_ready, t)
                    tt(y_rows[A, t - 1, :], x_rows[A, t - 1, :], t_ps[A, (t - 1) % 3, 0:D], ALU.add).then_inc(y_added, 1)

        @block.tensor
        def _(pe):
            mm = nc.tensor.matmul

            def turn_rows(n):
                pe.wait_ge(rows_ready, n)
                for t in range(TILES):
                    ins = nc.tensor.transpose(s_ps[:, t // QUARTER, (t % QUARTER) * D:(t % QUARTER) * D + ROWS],
                                              work[1][0:ROWS, t, :], ident[0:ROWS, 0:ROWS])
                ins.then_inc(rows_turned, 1)
                pe.wait_ge(rows_t_ready, n)

            pe.wait_ge(ident_set, 2)
            turn_rows(1)
            pe.wait_ge(w0_loaded, 32)
            for t in range(TILES):
                ins = mm(t_ps[0:ROWS, t // QUARTER, (t % QUARTER) * D:(t % QUARTER + 1) * D], rows_t[:, t, :], w0_sb,
                         start=True, stop=True)
            ins.then_inc(mx_ready, 1)
            pe.wait_ge(xt_ready, 1)
            pe.wait_ge(adj_loaded, 64)
            pe.wait_ge(ident_set, 4)
            for s in range(TILES):
                if s == 8:
                    pe.wait_ge(tile_max_ready, 1)
                    for i in range(TILES):
                        ins = nc.tensor.transpose(t_ps[0:ROWS, i // QUARTER, (i % QUARTER) * D:(i % QUARTER) * D + ROWS],
                                                  adj_tile_max[0:ROWS, i::TILES], ident[0:ROWS, 0:ROWS])
                    ins.then_inc(tile_max_turned, 1)
                for t in range(TILES):
                    k = ROWS if t == 0 else FULL
                    ins = mm(s_ps[0:ROWS, s // QUARTER, (s % QUARTER) * D:(s % QUARTER + 1) * D],
                             adj[0:k, t, s::TILES], work[1][0:k, t, :], start=t == 0, stop=t == TILES - 1)
            ins.then_inc(support_ready, 1)
            turn_rows(2)
            pe.wait_ge(row_max_ready, 1)
            pe.wait_ge(w_loaded, 48)

            def score_half(it, off, s, half, static_first):
                b = off % 2
                if s == 0 and half == 0:
                    pe.wait_ge(max_ops_loaded[b], turn(it, off) * 96 + 96)
                if not static_first:
                    pe.wait_ge(scores_maxed, head(it, off) * (2 * TILES) + 2 * s + half - 1)
                q = q_max[b][:, s::TILES]
                mm(s_slot[half][:, 0:BANK], q, k_max[b][:, half * HALF:half * HALF + BANK], start=True, stop=True)
                mm(s_slot[half][:, BANK:HALF], q, k_max[b][:, half * HALF + BANK:(half + 1) * HALF],
                   start=True, stop=True).then_inc(scores_ready, 1)

            def shifted_third(it, off, t, c):
                b = off % 2
                if t == 0 and c == 0:
                    pe.wait_ge(exp_ops_loaded[b], turn(it, off) * 96 + 96)
                    pe.wait_ge(neg_max_placed[b], turn(it, off) * 32 + 32)
                if t > 0 or exists(it, off - 1):
                    if c == 2:
                        pe.wait_ge(vec_probs, head(it, off) * TILES + t)
                    else:
                        pe.wait_ge(exp_done, head(it, off) * (3 * TILES) + 3 * t + c - 2)
                c0, w = EXP_COLS[c]
                ins = mm(t_ps[:, c, 0:w], k_exp[b][:, t::TILES], q_exp[b][:, c0:c0 + w], start=True, stop=c > 0 or not PEW)
                if c == 0 and PEW:
                    mm(t_ps[:, 0, 0:PEW], ident_h[0:ROWS, :], adj_parts[t][0:ROWS, 0, :], start=False, stop=False)
                    ins = mm(t_ps[:, 0, 0:PEW], ident_h[0:ROWS, :], adj_parts[t][0:ROWS, 1, :], start=False, stop=True)
                ins.then_inc(shifted_ready, 1)

            def weighted_sum(it, off, t):
                b = off % 2
                if t == 0:
                    pe.wait_ge(v_loaded[b], turn(it, off) * 32 + 32)
                    if exists(it, off - 1):
                        pe.wait_ge(sums_copied, head(it, off))
                pe.wait_ge(vec_probs, head(it, off) * TILES + t + 1)
                pe.wait_ge(pool_probs, head(it, off) * TILES + t + 1)
                for c, (c0, w) in enumerate(SUM_COLS):
                    ins = mm(o_ps[32 * c:32 * c + VROW, 0:w], v_sb[b][0:ROWS, t * VROW:(t + 1) * VROW],
                             probs[t][0:ROWS, c0:c0 + w], start=t == 0, stop=t == TILES - 1)
                ins.then_inc(tile_summed, 1)

            for k, (r0, n) in enumerate(BLOCKS):
                tiles = first_maxima(k)

                def project(c):
                    c_all = 6 * k + c
                    if c_all >= 4:
                        old_k, old_c = divmod(c_all - 4, 6)
                        if old_c < 4:
                            pe.wait_ge(low_done, 4 * old_k + old_c + 1)
                        else:
                            pe.wait_ge(high_done, c_all - 4 + 1)
                    w = wqk_sb[:, c * BANK:(c + 1) * BANK] if c < 4 else wv_sb[:, (c - 4) * BANK:(c - 3) * BANK]
                    mm(proj_bank[c_all % 4][0:n, :], row_t[:, r0:r0 + n], w, start=True, stop=True).then_inc(proj_done, 1)

                def score(i, half):
                    if i < len(tiles):
                        score_half(0, tiles[i] // TILES, tiles[i] % TILES, half, tiles[i] == 0)

                project(0)
                project(1)
                score(0, 0)
                project(2)
                project(3)
                score(0, 1)
                project(4)
                score(1, 0)
                project(5)
                score(1, 1)
            pe.wait_ge(low_done, 4 * len(BLOCKS))
            pe.wait_ge(high_done, 6 * len(BLOCKS))
            pe.wait_ge(adj_shifted, TILES)

            def head_steps(it, off):
                for i in range(TILES):
                    ahead, s = off + 1 + (i + LEAD) // TILES, (i + LEAD) % TILES
                    if exists(it, ahead):
                        score_half(it, ahead, s, 0, False)
                    shifted_third(it, off, i, 0)
                    shifted_third(it, off, i, 1)
                    if exists(it, ahead):
                        score_half(it, ahead, s, 1, False)
                    shifted_third(it, off, i, 2)
                    back = off if i >= LAG else off - 1
                    if exists(it, back):
                        weighted_sum(it, back, (i - LAG) % TILES)

            head_loop(pe, head_steps)
            for t in range(TILES - LAG, TILES):
                weighted_sum(HEADS // 2 - 1, 1, t)

            for t in range(TILES + 1):
                if t < TILES:
                    if t >= 2:
                        pe.wait_ge(o_t_low, t - 1)
                        pe.wait_ge(o_t_high, t - 1)
                    pe.wait_ge(normed_v, t + 1)
                    pe.wait_ge(normed_p, t + 1)
                    for h in range(H):
                        ins = nc.tensor.transpose(s_slot[t % 2][:, h * D:h * D + ROWS],
                                                  o_rows[0:ROWS, h, t * D:(t + 1) * D], ident[0:ROWS, 0:ROWS])
                    ins.then_inc(o_turned, 1)
                if t >= 1:
                    pe.wait_ge(o_t_low, t)
                    pe.wait_ge(o_t_high, t)
                    if t >= 4:
                        pe.wait_ge(y_added, t - 3)
                    for h in range(H):
                        ins = mm(t_ps[0:ROWS, (t - 1) % 3, 0:D], o_t[(t - 1) % 2][:, h, 0:ROWS], wo_sb[:, h * D:(h + 1) * D],
                                 start=h == 0, stop=h == H - 1)
                    ins.then_inc(y_ready, 1)


def kernel(x, adj, L0_gnn_weight, L0_gnn_bias, L1_gnn_Wq, L1_gnn_Wk, L1_gnn_Wv, L1_gnn_Wo):
    import numpy as np
    import concourse.bacc as bacc
    from concourse.bass_utils import run_bass_kernel_spmd

    def by_head(w):
        return np.asarray(w).reshape(D, H, D).transpose(2, 1, 0).reshape(D, C)

    arrays = {
        "x": np.asarray(x),
        "adj_t": np.asarray(adj).T,
        "w0_t": np.asarray(L0_gnn_weight).T,
        "bias": np.asarray(L0_gnn_bias).reshape(1, D),
        "wqk": np.concatenate([by_head(L1_gnn_Wq), by_head(L1_gnn_Wk)], axis=1),
        "wv": np.asarray(L1_gnn_Wv).T,
        "wo": np.asarray(L1_gnn_Wo).reshape(D, D, H).transpose(1, 2, 0).reshape(D, H * D),
    }
    arrays = {f"in_{n}": np.ascontiguousarray(a) for n, a in arrays.items()}
    nc = bacc.Bacc("TRN2", target_bir_lowering=False, num_devices=1)
    args = [nc.dram_tensor(n, a.shape, F32, kind="ExternalInput").ap() for n, a in arrays.items()]
    out = nc.dram_tensor("out", (N, D), F32, kind="ExternalOutput").ap()
    build_block(nc, *args, out)
    result = run_bass_kernel_spmd(nc, [arrays], core_ids=[0])
    return result.results[0]["out"]
```

```python
import concourse.bass as bass
from concourse import mybir
from contextlib import ExitStack

F32 = mybir.dt.float32
F16 = mybir.dt.float16
ALU = mybir.AluOpType
ACT = mybir.ActivationFunctionType
AX_X = mybir.AxisListType.X

N, D, H = 1354, 128, 8
P = 128
C = D * H
HEADS = D
FLAT = N * D
TILES = -(-N // P)
FULL = N // TILES
ROWS = FULL + 1
LASTROW = FULL * TILES
PADN = TILES * P
ADJW = TILES * ROWS
LN_EPS = 1e-5
LOWEST = -3e38
MIN_NORM = 1e-15
MAX_NORM = 1.0 - 0.004
ARTANH_CLIP = 1.0 - 2.0 ** -23
ARTANH_MAX_NORM = 3.1063029
SCALE = float(D) ** -0.5

BANK = 512
PAIRS = (N - BANK) // 2
SINGLES = N - 2 * PAIRS
PEW = 42
POOLW = 800
EDGES = (0, 512, PEW + POOLW, N)
EXP_COLS = [(a, b - a) for a, b in zip(EDGES, EDGES[1:])]
SUMW = 339
SUM_COLS = [(c * SUMW, min(SUMW, N - c * SUMW)) for c in range(4)]
VROW = H + 1
LEAD = 3
NEGATE_AT = 5
LAG = 4
BLOCKS = [(r, min(P, N - r)) for r in range(0, N, P)]
STAGES = 5
V_STAGES = 3
V_STAGES_END = 4448 + V_STAGES * D * VROW
FIRST_MAX = 3
EARLY = (HEADS - 2) * N // PADN
STAGED_FROM = (TILES * N - 3 * 2 * C) // N
QUARTER = BANK // D


def build_block(nc, x, adj_t, w0_t, bias, wqk, wv, wo, out):
    ctx = ExitStack()
    with ctx:
        def sb(name, shape, dt=F32):
            return ctx.enter_context(nc.sbuf_tensor(name, shape, dt))

        def ps(name, shape):
            return ctx.enter_context(nc.psum_tensor(name, shape, F32))

        def sem(name):
            return ctx.enter_context(nc.semaphore(name))

        q_split = nc.dram_tensor("q_split", (2 * H, FLAT), F16, kind="Internal").ap()
        k_split = nc.dram_tensor("k_split", (2 * H, FLAT), F16, kind="Internal").ap()
        v_rows = nc.dram_tensor("v_rows", (FLAT, VROW), F32, kind="Internal").ap()
        o_cols = nc.dram_tensor("o_cols", (VROW, FLAT), F32, kind="Internal").ap()
        adj_max_row = nc.dram_tensor("adj_max_row", (1, N), F32, kind="Internal").ap()

        adj_sb = sb("adj_sb", [P, TILES * ADJW])
        adj = adj_sb[:].rearrange("p (t n) -> p t n", t=TILES)
        ring = sb("ring", [P, TILES * N])
        probs = [ring[:, t * N:(t + 1) * N] for t in range(TILES)]
        rows_x = sb("rows_x", [P, TILES * D])
        shared = sb("shared", [P, VROW * PADN])
        wqk_sb, wv_sb = shared[:, 0:2 * C], shared[:, 2 * C:3 * C]
        row_t = shared[:, 3 * C:3 * C + ADJW]
        v_stage = shared[:, 4448:V_STAGES_END].rearrange("p (b c) -> p b c", b=V_STAGES)
        o_rows = shared[:].rearrange("p (h c) -> p h c", h=VROW)
        x_rows = rows_x[:].rearrange("p (t d) -> p t d", t=TILES)
        rows_t = row_t.rearrange("p (t r) -> p t r", t=TILES)
        rows_in_order = row_t.rearrange("p (r t) -> p t r", t=TILES)
        work = [ring[:, i * 1536:(i + 1) * 1536].rearrange("p (t d) -> p t d", d=D) for i in range(3)]
        adj_max_b = ring[:, 4608:4608 + N]
        adj_tile_max = ring[:, 6144:6144 + ADJW]
        w0_sb = ring[:, 7552:7552 + D]
        adj_part = ring[:, 7680:7680 + PEW]
        stage_words = 2 * C
        stage_at = [shared[:, VROW * PADN - stage_words:VROW * PADN],
                    *[ring[:, TILES * N - b * stage_words:TILES * N - (b - 1) * stage_words] for b in (1, 2, 3)],
                    shared[:, VROW * PADN - 2 * stage_words:VROW * PADN - stage_words]]
        stage = [s.bitcast(F16).rearrange("p (w r c) -> p w r c", w=2, r=2 * H) for s in stage_at]
        stat = sb("stat", [P, 13, TILES + 1])
        adj_parts = [adj[:, t, 0:PEW].bitcast(F16).rearrange("p (a n) -> p a n", a=2) for t in range(TILES)]
        ident_h = sb("ident_h", [P, P], F16)
        adj_row_max = sb("adj_row_max", [P, TILES])
        wo_sb = sb("wo_sb", [P, H * D])
        ident = sb("ident", [P, P])
        q_max = [sb(f"q_max{b}", [P, PADN], F16) for b in range(2)]
        k_max = [sb(f"k_max{b}", [P, N - PAIRS], F16) for b in range(2)]
        k_neg = [sb(f"k_neg{b}", [P, PAIRS], F16) for b in range(2)]
        sign = sb("sign", [P, 1])
        gate = sb("gate", [1, 1])
        diff = [sb("diff", [P, PAIRS])[:], shared[:, V_STAGES_END:V_STAGES_END + PAIRS]]
        q_exp = [sb(f"q_exp{b}", [P, PADN], F16) for b in range(2)]
        k_exp = [sb(f"k_exp{b}", [P, PADN], F16) for b in range(2)]
        v_sb = [sb(f"v_sb{b}", [P, TILES * VROW]) for b in range(2)]
        part_max = [sb(f"part_max{b}", [P, TILES, 2]) for b in range(2)]
        neg_max = [sb(f"neg_max{b}", [P, TILES], F16) for b in range(2)]
        o_sb = sb("o_sb", [P, SUMW])
        o_t = [ring[:, b * 1024:(b + 1) * 1024].rearrange("p (h r) -> p h r", h=H) for b in range(2)]
        recip_sum = ring[:, 2048:2048 + PADN]
        y_rows = ring[:, 4096:4096 + PADN].rearrange("p (t d) -> p t d", t=TILES)

        s_ps = ps("s_ps", [P, 4, BANK])
        t_ps = ps("t_ps", [P, 3, BANK])
        o_ps = ps("o_ps", [P, BANK])
        s_slot = [s_ps[:, 2 * b:2 * b + 2, :].rearrange("p b c -> p (b c)") for b in range(2)]
        diff_ps, sum_ps, single_ps = s_ps[:, 0, 0:PAIRS], s_ps[:, 1, 0:PAIRS], s_ps[:, 2, :]
        third_ps = [t_ps[:, 2, :], s_ps[:, 3, :]]
        proj_bank = [t_ps[:, b, :] for b in range(3)] + [o_ps[:]]

        x_loaded, w0_loaded, w_loaded, adj_loaded = sem("x_loaded"), sem("w0_loaded"), sem("w_loaded"), sem("adj_loaded")
        ident_set, pads_zeroed, pads_set = sem("ident_set"), sem("pads_zeroed"), sem("pads_set")
        dve_step, pool_step = sem("dve_step"), sem("pool_step")
        stat_ready, stat_done = sem("stat_ready"), sem("stat_done")
        rows_ready, rows_turned, rows_t_ready = sem("rows_ready"), sem("rows_turned"), sem("rows_t_ready")
        mx_ready, xt_ready, support_ready = sem("mx_ready"), sem("xt_ready"), sem("support_ready")
        tile_max_ready, tile_max_turned, row_max_ready = sem("tile_max_ready"), sem("tile_max_turned"), sem("row_max_ready")
        row_max_stored, row_max_loaded = sem("row_max_stored"), sem("row_max_loaded")
        adj_shifted, e_ready = sem("adj_shifted"), sem("e_ready")
        proj_done, high_done, low_done = sem("proj_done"), sem("high_done"), sem("low_done")
        qk_stored = [sem(f"qk_stored{b}") for b in range(STAGES)]
        v_stored = [sem(f"v_stored{b}") for b in range(V_STAGES)]
        max_ops_loaded = [sem(f"max_ops_loaded{b}") for b in range(2)]
        exp_ops_loaded = [sem(f"exp_ops_loaded{b}") for b in range(2)]
        v_loaded = [sem(f"v_loaded{b}") for b in range(2)]
        neg_max_placed = [sem(f"neg_max_placed{b}") for b in range(2)]
        k_neg_ready, diff_ready, abs_ready = sem("k_neg_ready"), sem("diff_ready"), sem("abs_ready")
        scores_ready, scores_maxed = sem("scores_ready"), sem("scores_maxed")
        neg_max_ready = sem("neg_max_ready")
        shifted_ready, exp_done = sem("shifted_ready"), sem("exp_done")
        vec_probs, pool_probs = sem("vec_probs"), sem("pool_probs")
        tile_summed, sums_copied = sem("tile_summed"), sem("sums_copied")
        sums_stored = [sem(f"sums_stored{b}") for b in range(2)]
        o_early, o_loaded, recip_ready, normed_v, normed_p = sem("o_early"), sem("o_loaded"), sem("recip_ready"), sem("normed_v"), sem("normed_p")
        o_turned, o_t_low, o_t_high, y_ready, y_added, out_stored = sem("o_turned"), sem("o_t_low"), sem("o_t_high"), sem("y_ready"), sem("y_added"), sem("out_stored")

        block = ctx.enter_context(nc.Block())

        def head_loop(eng, steps):
            for off in range(2):
                steps(0, off)
            with eng.Fori(1, HEADS // 2 - 1) as it:
                for off in range(2):
                    steps(it, off)
            for off in range(2):
                steps(HEADS // 2 - 1, off)

        def exists(it, off):
            return not isinstance(it, int) or 0 <= 2 * it + off < HEADS

        def head(it, off):
            return it * 2 + off

        def turn(it, off):
            return it + off // 2

        def flat_tiles(arr):
            return arr[:, 0:LASTROW * D].rearrange("r (p c) -> p r c", c=TILES * D)

        def first_maxima(block_number):
            u = 2 * (block_number - FIRST_MAX)
            return [v for v in (u, u + 1) if 0 <= v < TILES + LEAD]

        @block.sync
        def _(sp):
            sp.dma_start(x_rows[0:FULL, :, :], x[0:LASTROW, :].rearrange("(p t) d -> p t d", t=TILES)).then_inc(x_loaded, 16)
            sp.dma_start(x_rows[FULL:ROWS, :, :],
                         x[LASTROW:N, :].unsqueeze(1).to_broadcast([1, TILES, D])).then_inc(x_loaded, 16)
            sp.dma_start(w0_sb, w0_t).then_inc(w0_loaded, 16)
            sp.dma_start(work[0][0:ROWS, TILES, :], bias.to_broadcast([ROWS, D])).then_inc(w0_loaded, 16)
            for t0, t1 in ((0, 4), (4, 8), (8, TILES)):
                sp.dma_start(adj[0:FULL, t0:t1, 0:N],
                             adj_t[0:LASTROW, :].rearrange("(p t) n -> p t n", t=TILES)[:, t0:t1, :]).then_inc(adj_loaded, 16)
            sp.dma_start(adj[FULL:ROWS, :, 0:N],
                         adj_t[LASTROW:N, :].unsqueeze(1).to_broadcast([1, TILES, N])).then_inc(adj_loaded, 16)
            sp.dma_start(wqk_sb, wqk).then_inc(w_loaded, 16)
            sp.dma_start(wv_sb, wv).then_inc(w_loaded, 16)
            sp.dma_start(wo_sb[:], wo).then_inc(w_loaded, 16)

            sp.wait_ge(row_max_ready, 1)
            sp.dma_start(adj_max_row[0, 0:LASTROW].rearrange("(p t) -> p t", t=TILES), adj_row_max[0:FULL, :]).then_inc(row_max_stored, 16)
            sp.dma_start(adj_max_row[0:1, LASTROW:N], adj_row_max[FULL:ROWS, 0:1]).then_inc(row_max_stored, 16)
            sp.wait_ge(row_max_stored, 32)
            sp.dma_start(adj_max_b[0:ROWS, :], adj_max_row.to_broadcast([ROWS, N])).then_inc(row_max_loaded, 16)

            def load_operands(q_dst, k_dst, it, off, signal):
                cols = bass.ds(head(it, off) * N, N)
                for i in range(2):
                    sp.dma_start(q_dst[2 * H * i:2 * H * (i + 1), 0:N], q_split[:, cols]).then_inc(signal, 16)
                    for j in range(2):
                        r = 2 * H * i + H * j
                        sp.dma_start(k_dst[r:r + H, 0:N], k_split[H * i:H * (i + 1), cols]).then_inc(signal, 16)

            def load_max_operands(it, off):
                b, first = off % 2, head(it, off) * N
                for i in range(4):
                    sp.dma_start(q_max[b][2 * H * i:2 * H * (i + 1), 0:N], q_split[:, bass.ds(first, N)]).then_inc(max_ops_loaded[b], 16)
                for r in range(4):
                    parts = k_split[H * (r // 2):H * (r // 2 + 1), :]
                    sp.dma_start(k_max[b][H * r:H * (r + 1), :], parts[:, bass.ds(first + PAIRS, N - PAIRS)]).then_inc(max_ops_loaded[b], 16)
                    sp.dma_start(k_max[b][H * (4 + r):H * (5 + r), 0:PAIRS], parts[:, bass.ds(first, PAIRS)]).then_inc(max_ops_loaded[b], 16)

            def load_v(it, off):
                b, first = off % 2, head(it, off) * N
                src = v_rows[bass.ds(first, LASTROW), :].rearrange("(p t) c -> p (t c)", t=TILES)
                sp.dma_start(v_sb[b][0:FULL, :], src).then_inc(v_loaded[b], 16)
                sp.dma_start(v_sb[b][FULL:ROWS, 0:VROW], v_rows[bass.ds(first + LASTROW, 1), :]).then_inc(v_loaded[b], 16)

            def place_neg_max(b):
                sp.dma_start(q_exp[b][4 * H:4 * H + 1, 0:LASTROW], neg_max[b][0:FULL, :]).then_inc(neg_max_placed[b], 16)
                sp.dma_start(q_exp[b][4 * H:4 * H + 1, LASTROW:N], neg_max[b][FULL:ROWS, 0:1]).then_inc(neg_max_placed[b], 16)

            def store_sums(it, off):
                b = off % 2
                for c, (c0, w) in enumerate(SUM_COLS):
                    sp.dma_start(o_cols[:, bass.ds(head(it, off) * N + c0, w)],
                                 o_sb[32 * c:32 * c + VROW, 0:w]).then_inc(sums_stored[b], 16)

            v_by_row = v_rows.rearrange("(r j) c -> r (j c)", j=D)
            for k, (r0, n) in enumerate(BLOCKS):
                sp.wait_ge(low_done, 4 * (k + 1))
                for w, arr in enumerate((q_split, k_split)):
                    sp.dma_start(arr[:, r0 * D:(r0 + n) * D].rearrange("r (p j) -> p r j", j=D),
                                 stage[k % STAGES][0:n, w, :, :]).then_inc(qk_stored[k % STAGES], 16)
                sp.wait_ge(high_done, 6 * (k + 1))
                sp.dma_start(v_by_row[r0:r0 + n, :], v_stage[0:n, k % V_STAGES, :]).then_inc(v_stored[k % V_STAGES], 16)
                if k == FIRST_MAX + 5:
                    sp.wait_ge(neg_max_ready, 1)
                    place_neg_max(0)
                if k == 1:
                    sp.wait_ge(qk_stored[0], 32)
                    sp.wait_ge(v_stored[0], 16)
                    sp.wait_ge(pads_set, 1)
                    for off in range(2):
                        load_max_operands(0, off)
                    for off in range(2):
                        load_operands(q_exp[off], k_exp[off], 0, off, exp_ops_loaded[off])
                        load_v(0, off)
                if k == FIRST_MAX + 6:
                    sp.wait_ge(scores_ready, 2 * TILES)
                    load_max_operands(0, 2)
            for b in range(STAGES):
                sp.wait_ge(qk_stored[b], 32 * len(BLOCKS[b::STAGES]))
            for b in range(V_STAGES):
                sp.wait_ge(v_stored[b], 16 * len(BLOCKS[b::V_STAGES]))

            def head_steps(it, off):
                b = off % 2
                begun = isinstance(it, int) and it == off == 0
                if exists(it, off + 2) and not begun:
                    sp.wait_ge(scores_ready, head(it, off) * (2 * TILES) + 2 * TILES)
                    load_max_operands(it, off + 2)
                if exists(it, off + 1) and not begun:
                    if exists(it, off - 1):
                        sp.wait_ge(shifted_ready, head(it, off) * (3 * TILES))
                    load_operands(q_exp[1 - b], k_exp[1 - b], it, off + 1, exp_ops_loaded[1 - b])
                    if exists(it, off - 1):
                        sp.wait_ge(tile_summed, head(it, off) * TILES)
                    load_v(it, off + 1)
                if exists(it, off - 1):
                    sp.wait_ge(sums_copied, head(it, off))
                    store_sums(it, off - 1)
                if exists(it, off + 1):
                    sp.wait_ge(neg_max_ready, head(it, off) + 2)
                    place_neg_max(1 - b)

            head_loop(sp, head_steps)
            sp.wait_ge(sums_copied, HEADS)
            store_sums(HEADS // 2 - 1, 1)
            for b in range(2):
                sp.wait_ge(sums_stored[b], 64 * (HEADS // 2))

            sp.dma_start(o_rows[EARLY:FULL, :, :], flat_tiles(o_cols)[EARLY:FULL, :, :]).then_inc(o_loaded, 16)
            last = o_cols[:, LASTROW * D:FLAT].unsqueeze(0).unsqueeze(2).to_broadcast([1, VROW, TILES, D])
            sp.dma_start(o_rows[FULL:ROWS, :, :].rearrange("p h (t c) -> p h t c", t=TILES), last).then_inc(o_loaded, 16)
            half = TILES // 2 + 2
            out_rows = out[0:LASTROW, :].rearrange("(p t) d -> p t d", t=TILES)
            sp.wait_ge(y_added, half)
            sp.dma_start(out_rows[:, 0:half, :], y_rows[0:FULL, 0:half, :]).then_inc(out_stored, 16)
            sp.dma_start(out[LASTROW:N, :], y_rows[FULL:ROWS, 0, :]).then_inc(out_stored, 16)
            sp.wait_ge(y_added, TILES)
            sp.dma_start(out_rows[:, half:TILES, :], y_rows[0:FULL, half:TILES, :]).then_inc(out_stored, 16)
            sp.wait_ge(out_stored, 48)

        @block.gpsimd
        def _(pool):
            nc.gpsimd.memset(ident[:], 0.0).then_inc(ident_set, 1)
            pool.wait_ge(ident_set, 1)
            nc.gpsimd.affine_select(out=ident[:], in_=ident[:], compare_op=ALU.not_equal, fill=1.0,
                                    base=0, pattern=[[-1, P]], channel_multiplier=1).then_inc(ident_set, 1)
            pool.wait_ge(ident_set, 2)
            nc.gpsimd.tensor_copy(ident_h[:], ident[:]).then_inc(ident_set, 1)
            nc.gpsimd.memset(adj[:, :, N:ADJW], 0.0).then_inc(ident_set, 1)
            nc.gpsimd.memset(v_stage, 1.0).then_inc(ident_set, 1)
            for b in range(2):
                for buf in (q_max[b], k_neg[b], k_max[b], q_exp[b], k_exp[b], v_sb[b], part_max[b]):
                    nc.gpsimd.memset(buf[:], 0.0).then_inc(pads_zeroed, 1)
            pool.wait_ge(pads_zeroed, 14)
            nc.gpsimd.memset(k_exp[0][4 * H:4 * H + 1, 0:N], 1.0).then_inc(pads_zeroed, 1)
            nc.gpsimd.memset(sign[0:4 * H, :], 1.0).then_inc(pads_zeroed, 1)
            nc.gpsimd.memset(sign[4 * H:8 * H, :], -1.0).then_inc(pads_zeroed, 1)
            pool.wait_ge(pads_zeroed, 17)
            nc.gpsimd.memset(k_exp[1][4 * H:4 * H + 1, 0:N], 1.0).then_inc(pads_set, 1)

            links = [0]

            def link(ins):
                links[0] += 1
                ins.then_inc(pool_step, 1)
                pool.wait_ge(pool_step, links[0])

            tt = nc.gpsimd.tensor_tensor
            A = slice(0, ROWS)
            pool.wait_ge(pads_set, 1)
            pool.wait_ge(row_max_loaded, 16)
            pool.wait_ge(support_ready, 1)
            for t in range(TILES):
                high, low = adj_parts[t][A, 0, :], adj_parts[t][A, 1, :]
                link(tt(adj_part[A, :], adj[A, t, 0:PEW], adj_max_b[A, 0:PEW], ALU.subtract))
                link(nc.gpsimd.tensor_scalar(adj_part[A, :], adj_part[A, :], 2.0 / SCALE, None, ALU.mult))
                link(nc.gpsimd.tensor_copy(high, adj_part[A, :]))
                link(tt(low, adj_part[A, :], high, ALU.subtract))
                tt(adj[A, t, PEW:N], adj[A, t, PEW:N], adj_max_b[A, PEW:N], ALU.subtract).then_inc(adj_shifted, 1)
            pool.wait_ge(e_ready, TILES)

            def head_steps(it, off):
                for t in range(TILES):
                    pool.wait_ge(exp_done, head(it, off) * (3 * TILES) + 3 * t + 2)
                    cols = slice(PEW, PEW + POOLW)
                    nc.gpsimd.tensor_tensor(probs[t][0:ROWS, cols], probs[t][0:ROWS, cols], adj[0:ROWS, t, cols],
                                            ALU.mult).then_inc(pool_probs, 1)

            head_loop(pool, head_steps)
            for t in range(TILES):
                pool.wait_ge(recip_ready, t + 1)
                part = o_rows[A, H // 2:H, t * D:(t + 1) * D]
                tt(part, part, recip_sum[A, t * D:(t + 1) * D].unsqueeze(1).to_broadcast([ROWS, H // 2, D]),
                   ALU.mult).then_inc(normed_p, 1)

        @block.scalar
        def _(act):
            def row_stat(n, dst, src, func, **more):
                act.wait_ge(stat_ready, n)
                nc.scalar.activation(dst, src, func, **more).then_inc(stat_done, 1)

            A = slice(0, ROWS)
            row_stat(1, stat[A, 2, 0:TILES], stat[A, 1, 0:TILES], ACT.Sqrt)
            row_stat(2, stat[A, 1, 0:TILES], stat[A, 0, 0:TILES], ACT.Sqrt)
            row_stat(3, stat[A, 3, :], stat[A, 2, :], ACT.Sqrt)
            row_stat(4, stat[A, 8, 0:TILES], stat[A, 7, 0:TILES], ACT.Ln)
            row_stat(5, stat[A, 9, :], stat[A, 8, :], ACT.Tanh)
            row_stat(6, stat[A, 1, 0:TILES], stat[A, 0, 0:TILES], ACT.Sqrt)
            row_stat(7, stat[A, 8, 0:TILES], stat[A, 7, 0:TILES], ACT.Ln)
            row_stat(8, stat[A, 1, 0:TILES], stat[A, 0, 0:TILES], ACT.Sqrt)
            row_stat(9, stat[A, 1, 0:TILES], stat[A, 0, 0:TILES], ACT.Sqrt)
            row_stat(10, stat[A, 3, 0:TILES], stat[A, 2, 0:TILES], ACT.Tanh)
            row_stat(11, stat[A, 2, 0:TILES], stat[A, 1, 0:TILES], ACT.Sqrt)

            def abs_diff(it, off, s):
                act.wait_ge(diff_ready, head(it, off) * TILES + s + 1)
                if s > 1 or exists(it, off - 1):
                    act.wait_ge(scores_maxed, head(it, off) * (2 * TILES) + 2 * s - 2)
                nc.scalar.activation(diff[(off * TILES + s) % 2], diff_ps, ACT.Abs).then_inc(abs_ready, 1)

            act.wait_ge(ident_set, 5)
            c_all = 0
            for k, (r0, n) in enumerate(BLOCKS):
                if k >= STAGES:
                    act.wait_ge(qk_stored[k % STAGES], 32 * (k // STAGES))
                if k >= V_STAGES:
                    act.wait_ge(v_stored[k % V_STAGES], 16 * (k // V_STAGES))
                for c in range(6):
                    if c in (2, 4) and c // 2 - 1 < len(first_maxima(k)):
                        tile = first_maxima(k)[c // 2 - 1]
                        abs_diff(0, tile // TILES, tile % TILES)
                    act.wait_ge(proj_done, c_all + 1)
                    src = proj_bank[c_all % 4][0:n, :]
                    if c < 4:
                        dst = stage[k % STAGES][0:n, c // 2, 4 * (c % 2):4 * (c % 2) + 4, :]
                        src = src.rearrange("p (h j) -> p h j", j=D)
                    else:
                        dst = v_stage[0:n, k % V_STAGES, (c - 4) * 64 * VROW:(c - 3) * 64 * VROW].rearrange("p (j k) -> p j k", k=VROW)[:, :, 0:H]
                        src = src.rearrange("p (j k) -> p j k", k=H)
                    nc.scalar.activation(dst, src, ACT.Copy).then_inc(high_done, 1)
                    c_all += 1
                act.wait_ge(adj_shifted, k + 1)
                nc.scalar.activation(adj[A, k, PEW:N], adj[A, k, PEW:N], ACT.Exp, scale=2.0).then_inc(e_ready, 1)

            def head_steps(it, off):
                b = off % 2
                for i in range(TILES):
                    ahead, s = off + 1 + (i + LEAD) // TILES, (i + LEAD) % TILES
                    if isinstance(it, int) and it == off == 0 and i == STAGED_FROM:
                        for b in range(STAGES):
                            act.wait_ge(qk_stored[b], 32 * len(BLOCKS[b::STAGES]))
                    if exists(it, off - 1):
                        act.wait_ge(tile_summed, head(it, off) * TILES + (i + 1 - TILES))
                    if i == LAG and exists(it, off - 1):
                        copy_sums(it, off - 1)
                    for c, (c0, w) in enumerate(EXP_COLS):
                        if c == 2 and exists(it, ahead):
                            abs_diff(it, ahead, s)
                        act.wait_ge(shifted_ready, head(it, off) * (3 * TILES) + 3 * i + c + 1)
                        src = third_ps[(off * TILES + i) % 2] if c == 2 else t_ps[:, c, :]
                        dst = src[A, 0:w] if c == 2 else probs[i][A, c0:c0 + w]
                        nc.scalar.activation(dst, src[A, 0:w], ACT.Exp, scale=SCALE).then_inc(exp_done, 1)
                    if not exists(it, off + 1) and i == 1:
                        bring_back_sums()

            def copy_sums(it, off):
                b = off % 2
                act.wait_ge(tile_summed, head(it, off) * TILES + TILES)
                if exists(it, off - 1):
                    act.wait_ge(sums_stored[1 - b], turn(it, off - 1) * 64 + 64)
                nc.scalar.activation(o_sb[:], o_ps[:, 0:SUMW], ACT.Copy).then_inc(sums_copied, 1)

            def bring_back_sums():
                for b in range(2):
                    act.wait_ge(sums_stored[b], 64 * (HEADS // 2 - 1))
                for h in range(VROW):
                    act.dma_start(o_rows[0:EARLY, h, :], flat_tiles(o_cols)[0:EARLY, h, :]).then_inc(o_early, 16)

            head_loop(act, head_steps)
            copy_sums(HEADS // 2 - 1, 1)
            for t in range(TILES):
                act.wait_ge(o_turned, t + 1)
                if t >= 2:
                    act.wait_ge(y_ready, t - 1)
                nc.scalar.activation(o_t[t % 2][:, 0:4, 0:ROWS], s_ps[:, 2 * (t % 2), :].rearrange("p (h r) -> p h r", r=D)[:, :, 0:ROWS],
                                     ACT.Copy).then_inc(o_t_low, 1)

        @block.vector
        def _(dve):
            steps = [0]
            asked = [0]

            def link(ins):
                steps[0] += 1
                ins.then_inc(dve_step, 1)
                dve.wait_ge(dve_step, steps[0])

            def ask(ins):
                asked[0] += 1
                ins.then_inc(stat_ready, 1)
                dve.wait_ge(stat_done, asked[0])

            A = slice(0, ROWS)
            tt, ts, stt = nc.vector.tensor_tensor, nc.vector.tensor_scalar, nc.vector.scalar_tensor_tensor

            def st(i, n=TILES):
                return stat[A, i, 0:n]

            def wide(i, n=TILES):
                return st(i, n).unsqueeze(2).to_broadcast([ROWS, n, D])

            def layernorm_relu(src, dst, centred, square):
                link(nc.vector.reduce_sum(st(0), src, AX_X))
                link(ts(st(0), st(0), -1.0 / D, None, ALU.mult))
                link(tt(centred, src, wide(0), ALU.add))
                link(tt(square, centred, centred, ALU.mult))
                link(nc.vector.reduce_sum(st(1), square, AX_X))
                ask(ts(st(1), st(1), 1.0 / D, LN_EPS, ALU.mult, ALU.add))
                link(nc.vector.reciprocal(st(2), st(2)))
                return stt(out=dst, in0=centred, scalar=0.0, in1=wide(2), op0=ALU.max, op1=ALU.mult)

            def artanh(dst, z):
                link(ts(st(4), st(z), 1.0, None, ALU.add))
                link(ts(st(5), st(z), -1.0, 1.0, ALU.mult, ALU.add))
                link(nc.vector.reciprocal(st(6), st(5)))
                ask(tt(st(7), st(4), st(6), ALU.mult))
                link(tt(st(4), st(z), st(z), ALU.mult))
                link(ts(st(5), st(4), 1.0 / 7, 1.0 / 5, ALU.mult, ALU.add))
                link(tt(st(5), st(5), st(4), ALU.mult))
                link(ts(st(5), st(5), 1.0 / 3, None, ALU.add))
                link(tt(st(5), st(5), st(4), ALU.mult))
                link(ts(st(5), st(5), 1.0, None, ALU.add))
                link(tt(st(5), st(5), st(z), ALU.mult))
                link(ts(st(8), st(8), 0.5, None, ALU.mult))
                link(ts(st(6), st(z), 0.1, None, ALU.is_lt))
                link(tt(st(5), st(5), st(8), ALU.subtract))
                link(tt(st(5), st(5), st(6), ALU.mult))
                link(tt(st(dst), st(8), st(5), ALU.add))

            dve.wait_ge(x_loaded, 32)
            h0 = work[1][A, 0:TILES, :]
            sq = work[2][A, 0:TILES, :]
            layernorm_relu(x_rows[A], h0, h0, sq).then_inc(rows_ready, 1)
            dve.wait_ge(rows_ready, 1)
            link(tt(sq, h0, h0, ALU.mult))
            ask(nc.vector.reduce_sum(st(0), sq, AX_X))
            link(ts(st(10), st(1), MIN_NORM, None, ALU.max))
            dve.wait_ge(rows_turned, 1)
            for b in range(3):
                k = min(QUARTER, TILES - QUARTER * b)
                ins = nc.vector.tensor_copy(rows_t[:, QUARTER * b:QUARTER * b + k, :],
                                            s_ps[:, b, 0:k * D].rearrange("p (t r) -> p t r", r=D)[:, :, 0:ROWS])
            ins.then_inc(rows_t_ready, 1)

            dve.wait_ge(w0_loaded, 32)
            dve.wait_ge(mx_ready, 1)
            for b in range(3):
                k = min(QUARTER, TILES - QUARTER * b)
                link(nc.vector.tensor_copy(work[0][A, QUARTER * b:QUARTER * b + k, :],
                                           t_ps[A, b, 0:k * D].rearrange("p (t d) -> p t d", d=D)))
            ALLR = TILES + 1
            mx = work[0][A, 0:ALLR, :]
            sqa = work[2][A, 0:ALLR, :]
            link(tt(sqa, mx, mx, ALU.mult))
            ask(nc.vector.reduce_sum(st(2, ALLR), sqa, AX_X))
            link(ts(st(3, ALLR), st(3, ALLR), MIN_NORM, None, ALU.max))
            link(ts(st(11), st(10), ARTANH_CLIP, None, ALU.min))
            artanh(12, 11)
            link(nc.vector.reciprocal(st(4), st(10)))
            link(tt(st(4), st(4), st(3), ALU.mult))
            link(tt(st(8), st(4), st(12), ALU.mult))
            ask(nc.vector.tensor_copy(stat[A, 8, TILES:ALLR], stat[A, 3, TILES:ALLR]))
            link(ts(st(9, ALLR), st(9, ALLR), MAX_NORM, None, ALU.min))
            link(nc.vector.reciprocal(st(4, ALLR), st(3, ALLR)))
            link(tt(st(4, ALLR), st(4, ALLR), st(9, ALLR), ALU.mult))
            link(tt(mx, mx, wide(4, ALLR), ALU.mult))
            res, hyp_bias = work[0][A, 0:TILES, :], work[0][A, TILES:ALLR, :].to_broadcast([ROWS, TILES, D])
            link(tt(sqa, mx, mx, ALU.mult))
            link(nc.vector.reduce_sum(st(5, ALLR), sqa, AX_X))
            link(tt(sq, res, hyp_bias, ALU.mult))
            link(nc.vector.reduce_sum(st(6), sq, AX_X))
            y2 = stat[A, 5, TILES:ALLR]
            link(ts(st(6), st(6), 2.0, 1.0, ALU.mult, ALU.add))
            link(ts(st(7), st(6), y2, None, ALU.add))
            link(ts(st(8), st(5), y2, None, ALU.mult))
            link(tt(st(8), st(8), st(6), ALU.add))
            link(ts(st(8), st(8), MIN_NORM, None, ALU.max))
            link(nc.vector.reciprocal(st(8), st(8)))
            link(ts(st(9), st(5), -1.0, 1.0, ALU.mult, ALU.add))
            link(tt(st(7), st(7), st(8), ALU.mult))
            link(tt(st(9), st(9), st(8), ALU.mult))
            link(tt(sq, res, wide(7), ALU.mult))
            link(tt(h0, hyp_bias, wide(9), ALU.mult))
            link(tt(h0, h0, sq, ALU.add))
            link(tt(sq, h0, h0, ALU.mult))
            ask(nc.vector.reduce_sum(st(0), sq, AX_X))
            link(ts(st(10), st(1), MIN_NORM, None, ALU.max))
            link(ts(st(11), st(10), MAX_NORM, None, ALU.min))
            artanh(12, 11)
            link(nc.vector.reciprocal(st(4), st(10)))
            link(tt(st(4), st(4), st(12), ALU.mult))
            tt(h0, h0, wide(4), ALU.mult).then_inc(xt_ready, 1)

            dve.wait_ge(adj_loaded, 64)
            dve.wait_ge(ident_set, 4)
            nc.vector.tensor_reduce(adj_tile_max[A, :], adj[A, :, :].rearrange("p t n -> p n t"),
                                    AX_X, ALU.max).then_inc(tile_max_ready, 1)
            dve.wait_ge(tile_max_turned, 1)
            for b in range(3):
                k = min(QUARTER, TILES - QUARTER * b)
                ins = nc.vector.tensor_reduce(adj_row_max[A, QUARTER * b:QUARTER * b + k],
                                              t_ps[A, b, 0:k * D].rearrange("p (t m) -> p t m", m=D)[:, :, 0:ROWS],
                                              AX_X, ALU.max)
                if b < 2:
                    link(ins)
            ins.then_inc(row_max_ready, 1)

            dve.wait_ge(support_ready, 1)
            sup = work[0][A, 0:TILES, :]
            for b in range(3):
                k = min(QUARTER, TILES - QUARTER * b)
                link(nc.vector.tensor_copy(work[0][A, QUARTER * b:QUARTER * b + k, :],
                                           s_ps[A, b, 0:k * D].rearrange("p (t d) -> p t d", d=D)))
            link(tt(sq, sup, sup, ALU.mult))
            ask(nc.vector.reduce_sum(st(0), sq, AX_X))
            link(ts(st(1), st(1), MIN_NORM, None, ALU.max))
            link(nc.vector.reciprocal(st(2), st(1)))
            link(ts(st(1), st(1), ARTANH_MAX_NORM, None, ALU.min))
            link(tt(st(1), st(1), st(2), ALU.mult))
            link(stt(out=sup, in0=sup, scalar=0.0, in1=wide(1), op0=ALU.max, op1=ALU.mult))
            link(tt(sq, sup, sup, ALU.mult))
            ask(nc.vector.reduce_sum(st(0), sq, AX_X))
            ask(ts(st(2), st(1), MIN_NORM, None, ALU.max))
            link(ts(st(3), st(3), MAX_NORM, None, ALU.min))
            link(nc.vector.reciprocal(st(2), st(2)))
            link(tt(st(2), st(2), st(3), ALU.mult))
            link(tt(sup, sup, wide(2), ALU.mult))
            link(tt(x_rows[A], x_rows[A], sup, ALU.add))

            layernorm_relu(x_rows[A], h0, h0, sq).then_inc(rows_ready, 1)
            dve.wait_ge(rows_turned, 2)
            for b in range(3):
                k = min(QUARTER, TILES - QUARTER * b)
                ins = nc.vector.tensor_copy(rows_in_order[:, QUARTER * b:QUARTER * b + k, :],
                                            s_ps[:, b, 0:k * D].rearrange("p (t r) -> p t r", r=D)[:, :, 0:ROWS])
            ins.then_inc(rows_t_ready, 1)

            def negate(it, off):
                b = off % 2
                dve.wait_ge(max_ops_loaded[b], turn(it, off) * 192 + 192)
                nc.vector.tensor_scalar(k_neg[b][0:8 * H, :], k_max[b][0:8 * H, 0:PAIRS], sign[0:8 * H, :], None,
                                        ALU.mult).then_inc(k_neg_ready, 1)

            def part_maximum(it, off, s, part):
                b = off % 2
                dve.wait_ge(scores_ready, head(it, off) * (2 * TILES) + 2 * s + part + 1)
                if part == 1:
                    dve.wait_ge(abs_ready, head(it, off) * TILES + s + 1)
                    nc.vector.memset(gate[:], 0.0)
                    d = diff[(off * TILES + s) % 2]
                    nc.vector.tensor_tensor_reduce(out=d, in0=sum_ps, in1=d, scale=0.5, scalar=LOWEST, op0=ALU.add, op1=ALU.max,
                                                   accum_out=part_max[b][:, s, 0:1]).then_inc(scores_maxed, 1)
                else:
                    nc.vector.reduce_max(part_max[b][:, s, 1:2], single_ps, AX_X).then_inc(scores_maxed, 1)

            def join_parts(it, off):
                b = off % 2
                dve.wait_ge(scores_maxed, head(it, off) * (2 * TILES) + 2 * TILES)
                if exists(it, off - 2):
                    dve.wait_ge(neg_max_placed[b], turn(it, off) * 32)
                nc.vector.tensor_reduce(neg_max[b][:], part_max[b][:], AX_X, ALU.max, negate=True).then_inc(neg_max_ready, 1)

            def product(it, off, t):
                if exists(it, off - 1):
                    dve.wait_ge(tile_summed, head(it, off) * TILES + (t + 1 - TILES))
                dve.wait_ge(exp_done, head(it, off) * (3 * TILES) + 3 * (t + 1))
                c0, w = EXP_COLS[2]
                nc.vector.tensor_tensor(probs[t][A, c0:c0 + w], third_ps[(off * TILES + t) % 2][A, 0:w], adj[A, t, c0:c0 + w],
                                        ALU.mult).then_inc(vec_probs, 1)

            for k, (r0, n) in enumerate(BLOCKS):
                tiles = first_maxima(k)

                def low(c):
                    c_all = 6 * k + c
                    dve.wait_ge(high_done, c_all + 1)
                    r = 4 * (c % 2)
                    tt(stage[k % STAGES][0:n, c // 2, H + r:H + r + 4, :],
                       proj_bank[c_all % 4][0:n, :].rearrange("p (h j) -> p h j", j=D),
                       stage[k % STAGES][0:n, c // 2, r:r + 4, :], ALU.subtract).then_inc(low_done, 1)

                def maximum(i, part):
                    if i < len(tiles):
                        if tiles[i] == 0 and part == 0:
                            dve.wait_ge(pads_set, 1)
                            for off in range(2):
                                negate(0, off)
                        part_maximum(0, tiles[i] // TILES, tiles[i] % TILES, part)
                        if tiles[i] % TILES == TILES - 1 and part == 1:
                            join_parts(0, 0)

                low(0)
                low(1)
                maximum(0, 0)
                low(2)
                low(3)
                maximum(0, 1)
                maximum(1, 0)
                maximum(1, 1)
            dve.wait_ge(e_ready, TILES)

            def head_steps(it, off):
                for i in range(TILES):
                    ahead, s = off + 1 + (i + LEAD) // TILES, (i + LEAD) % TILES
                    for part in range(2):
                        if exists(it, ahead):
                            part_maximum(it, ahead, s, part)
                    product(it, off, i)
                    if i == NEGATE_AT and exists(it, off + 2):
                        negate(it, off + 2)
                    if s == TILES - 1 and exists(it, ahead):
                        join_parts(it, ahead)

            head_loop(dve, head_steps)

            dve.wait_ge(o_early, 16 * VROW)
            dve.wait_ge(o_loaded, 32)

            def normalise(t):
                cols = slice(t * D, (t + 1) * D)
                nc.vector.reciprocal(recip_sum[A, cols], o_rows[A, H, cols]).then_inc(recip_ready, 1)
                dve.wait_ge(recip_ready, t + 1)
                part = o_rows[A, 0:H // 2, cols]
                tt(part, part, recip_sum[A, cols].unsqueeze(1).to_broadcast([ROWS, H // 2, D]), ALU.mult).then_inc(normed_v, 1)

            normalise(0)
            normalise(1)
            for t in range(TILES + 1):
                if t < TILES:
                    if t >= 2:
                        dve.wait_ge(y_ready, t - 1)
                    dve.wait_ge(o_turned, t + 1)
                    nc.vector.tensor_copy(o_t[t % 2][:, 4:8, 0:ROWS],
                                          s_ps[:, 2 * (t % 2) + 1, :].rearrange("p (h r) -> p h r", r=D)[:, :, 0:ROWS]).then_inc(o_t_high, 1)
                    if t + 2 < TILES:
                        normalise(t + 2)
                if t >= 1:
                    dve.wait_ge(y_ready, t)
                    tt(y_rows[A, t - 1, :], x_rows[A, t - 1, :], t_ps[A, (t - 1) % 3, 0:D], ALU.add).then_inc(y_added, 1)

        @block.tensor
        def _(pe):
            mm = nc.tensor.matmul

            def turn_rows(n):
                pe.wait_ge(rows_ready, n)
                for t in range(TILES):
                    ins = nc.tensor.transpose(s_ps[:, t // QUARTER, (t % QUARTER) * D:(t % QUARTER) * D + ROWS],
                                              work[1][0:ROWS, t, :], ident[0:ROWS, 0:ROWS])
                ins.then_inc(rows_turned, 1)
                pe.wait_ge(rows_t_ready, n)

            pe.wait_ge(ident_set, 2)
            turn_rows(1)
            pe.wait_ge(w0_loaded, 32)
            for t in range(TILES):
                ins = mm(t_ps[0:ROWS, t // QUARTER, (t % QUARTER) * D:(t % QUARTER + 1) * D], rows_t[:, t, :], w0_sb,
                         start=True, stop=True)
            ins.then_inc(mx_ready, 1)
            pe.wait_ge(xt_ready, 1)
            pe.wait_ge(adj_loaded, 64)
            pe.wait_ge(ident_set, 4)
            for s in range(TILES):
                if s == 8:
                    pe.wait_ge(tile_max_ready, 1)
                    for i in range(TILES):
                        ins = nc.tensor.transpose(t_ps[0:ROWS, i // QUARTER, (i % QUARTER) * D:(i % QUARTER) * D + ROWS],
                                                  adj_tile_max[0:ROWS, i::TILES], ident[0:ROWS, 0:ROWS])
                    ins.then_inc(tile_max_turned, 1)
                for t in range(TILES):
                    k = ROWS if t == 0 else FULL
                    ins = mm(s_ps[0:ROWS, s // QUARTER, (s % QUARTER) * D:(s % QUARTER + 1) * D],
                             adj[0:k, t, s::TILES], work[1][0:k, t, :], start=t == 0, stop=t == TILES - 1)
            ins.then_inc(support_ready, 1)
            turn_rows(2)
            pe.wait_ge(row_max_ready, 1)
            pe.wait_ge(w_loaded, 48)

            def score_part(it, off, s, part, static_first):
                b = off % 2
                q = q_max[b][:, s::TILES]
                if part == 0 and s == 0:
                    pe.wait_ge(max_ops_loaded[b], turn(it, off) * 192 + 192)
                if part == 1:
                    if s == 0:
                        pe.wait_ge(k_neg_ready, head(it, off) + 1)
                    if not static_first:
                        pe.wait_ge(abs_ready, head(it, off) * TILES + s)
                    mm(diff_ps, q, k_neg[b][:], start=True, stop=True).then_inc(diff_ready, 1)
                if not static_first:
                    pe.wait_ge(scores_maxed, head(it, off) * (2 * TILES) + 2 * s + part - 1)
                if part == 1:
                    mm(sum_ps, q, k_max[b][:, 0:PAIRS], start=True, stop=True).then_inc(scores_ready, 1)
                else:
                    mm(single_ps, q, k_max[b][:, PAIRS:N - PAIRS], start=True, stop=True).then_inc(scores_ready, 1)

            def shifted_third(it, off, t, c):
                b = off % 2
                if t == 0 and c == 0:
                    pe.wait_ge(exp_ops_loaded[b], turn(it, off) * 96 + 96)
                    pe.wait_ge(neg_max_placed[b], turn(it, off) * 32 + 32)
                if c == 2:
                    if t > 1 or exists(it, off - 1):
                        pe.wait_ge(vec_probs, head(it, off) * TILES + t - 1)
                elif t > 0 or exists(it, off - 1):
                    pe.wait_ge(exp_done, head(it, off) * (3 * TILES) + 3 * t + c - 2)
                c0, w = EXP_COLS[c]
                bank = third_ps[(off * TILES + t) % 2] if c == 2 else t_ps[:, c, :]
                ins = mm(bank[:, 0:w], k_exp[b][:, t::TILES], q_exp[b][:, c0:c0 + w], start=True, stop=c > 0 or not PEW)
                if c == 0 and PEW:
                    mm(t_ps[:, 0, 0:PEW], ident_h[0:ROWS, :], adj_parts[t][0:ROWS, 0, :], start=False, stop=False)
                    ins = mm(t_ps[:, 0, 0:PEW], ident_h[0:ROWS, :], adj_parts[t][0:ROWS, 1, :], start=False, stop=True)
                ins.then_inc(shifted_ready, 1)

            def weighted_sum(it, off, t):
                b = off % 2
                if t == 0:
                    pe.wait_ge(v_loaded[b], turn(it, off) * 32 + 32)
                    if exists(it, off - 1):
                        pe.wait_ge(sums_copied, head(it, off))
                pe.wait_ge(vec_probs, head(it, off) * TILES + t + 1)
                pe.wait_ge(pool_probs, head(it, off) * TILES + t + 1)
                for c, (c0, w) in enumerate(SUM_COLS):
                    ins = mm(o_ps[32 * c:32 * c + VROW, 0:w], v_sb[b][0:ROWS, t * VROW:(t + 1) * VROW],
                             probs[t][0:ROWS, c0:c0 + w], start=t == 0, stop=t == TILES - 1)
                ins.then_inc(tile_summed, 1)

            for k, (r0, n) in enumerate(BLOCKS):
                tiles = first_maxima(k)

                def project(c):
                    c_all = 6 * k + c
                    if c_all >= 4:
                        old_k, old_c = divmod(c_all - 4, 6)
                        if old_c < 4:
                            pe.wait_ge(low_done, 4 * old_k + old_c + 1)
                        else:
                            pe.wait_ge(high_done, c_all - 4 + 1)
                    w = wqk_sb[:, c * BANK:(c + 1) * BANK] if c < 4 else wv_sb[:, (c - 4) * BANK:(c - 3) * BANK]
                    mm(proj_bank[c_all % 4][0:n, :], row_t[:, r0:r0 + n], w, start=True, stop=True).then_inc(proj_done, 1)

                def score(i, part):
                    if i < len(tiles):
                        score_part(0, tiles[i] // TILES, tiles[i] % TILES, part, tiles[i] == 0)

                project(0)
                project(1)
                score(0, 0)
                project(2)
                project(3)
                score(0, 1)
                project(4)
                score(1, 0)
                project(5)
                score(1, 1)
            pe.wait_ge(low_done, 4 * len(BLOCKS))
            pe.wait_ge(high_done, 6 * len(BLOCKS))
            pe.wait_ge(adj_shifted, TILES)

            def head_steps(it, off):
                for i in range(TILES):
                    ahead, s = off + 1 + (i + LEAD) // TILES, (i + LEAD) % TILES
                    back = off if i >= LAG else off - 1
                    shifted_third(it, off, i, 0)
                    shifted_third(it, off, i, 1)
                    for part in range(2):
                        if exists(it, ahead):
                            score_part(it, ahead, s, part, False)
                    shifted_third(it, off, i, 2)
                    if exists(it, back):
                        weighted_sum(it, back, (i - LAG) % TILES)

            head_loop(pe, head_steps)
            for t in range(TILES - LAG, TILES):
                weighted_sum(HEADS // 2 - 1, 1, t)

            for t in range(TILES + 1):
                if t < TILES:
                    if t >= 2:
                        pe.wait_ge(o_t_low, t - 1)
                        pe.wait_ge(o_t_high, t - 1)
                    pe.wait_ge(normed_v, t + 1)
                    pe.wait_ge(normed_p, t + 1)
                    for h in range(H):
                        ins = nc.tensor.transpose(s_slot[t % 2][:, h * D:h * D + ROWS],
                                                  o_rows[0:ROWS, h, t * D:(t + 1) * D], ident[0:ROWS, 0:ROWS])
                    ins.then_inc(o_turned, 1)
                if t >= 1:
                    pe.wait_ge(o_t_low, t)
                    pe.wait_ge(o_t_high, t)
                    if t >= 4:
                        pe.wait_ge(y_added, t - 3)
                    for h in range(H):
                        ins = mm(t_ps[0:ROWS, (t - 1) % 3, 0:D], o_t[(t - 1) % 2][:, h, 0:ROWS], wo_sb[:, h * D:(h + 1) * D],
                                 start=h == 0, stop=h == H - 1)
                    ins.then_inc(y_ready, 1)


def kernel(x, adj, L0_gnn_weight, L0_gnn_bias, L1_gnn_Wq, L1_gnn_Wk, L1_gnn_Wv, L1_gnn_Wo):
    import numpy as np
    import concourse.bacc as bacc
    from concourse.bass_utils import run_bass_kernel_spmd

    def by_head(w):
        return np.asarray(w).reshape(D, H, D).transpose(2, 1, 0).reshape(D, C)

    arrays = {
        "x": np.asarray(x),
        "adj_t": np.asarray(adj).T,
        "w0_t": np.asarray(L0_gnn_weight).T,
        "bias": np.asarray(L0_gnn_bias).reshape(1, D),
        "wqk": np.concatenate([by_head(L1_gnn_Wq), by_head(L1_gnn_Wk)], axis=1),
        "wv": np.asarray(L1_gnn_Wv).T,
        "wo": np.asarray(L1_gnn_Wo).reshape(D, D, H).transpose(1, 2, 0).reshape(D, H * D),
    }
    arrays = {f"in_{n}": np.ascontiguousarray(a) for n, a in arrays.items()}
    nc = bacc.Bacc("TRN2", target_bir_lowering=False, num_devices=1)
    args = [nc.dram_tensor(n, a.shape, F32, kind="ExternalInput").ap() for n, a in arrays.items()]
    out = nc.dram_tensor("out", (N, D), F32, kind="ExternalOutput").ap()
    build_block(nc, *args, out)
    result = run_bass_kernel_spmd(nc, [arrays], core_ids=[0])
    return result.results[0]["out"]
```
